# Optimizing a Trainium2 kernel written in Bass

```python
import numpy as np
import jax
import jax.numpy as jnp

def _softmax(x, axis=-1):
    return jax.nn.softmax(x, axis=axis)

def _gelu(x):
    return jax.nn.gelu(x, approximate=True)

def _silu(x):
    return jax.nn.silu(x)

def _sigmoid(x):
    return jax.nn.sigmoid(x)

def _layernorm(x, axis=-1, eps=1e-05):
    m = jnp.mean(x, axis=axis, keepdims=True)
    v = jnp.var(x, axis=axis, keepdims=True)
    return (x - m) / jnp.sqrt(v + eps)

def _scatter_add(tgt, idx, src, axis=0):
    return tgt.at[idx].add(src)

def _segment_sum(src, seg, n):
    return jax.ops.segment_sum(src, seg, n)
kernel_name = 'mk_seq_postln_d1_jaxref_r8_caba97'

def setup_inputs(seed: int=0):
    np.random.seed(seed)
    _w = jnp.asarray

    def _L0_attn_setup():
        import jax, jax.numpy as jnp
        import numpy as np
        B, N, E, H = (2, 256, 128, 16)
        D = E // H
        LN_EPS = 1e-05
        key = jax.random.key(seed)
        k1, k2 = jax.random.split(key)
        x = jax.random.normal(k1, (B, N, E), dtype=jnp.float32)
        gamma = jnp.ones((E,), dtype=jnp.float32)
        beta = jnp.zeros((E,), dtype=jnp.float32)
        w_qkv = jax.random.normal(k2, (3 * E, E), dtype=jnp.float32) * E ** (-0.5)
        return {'x': x, 'gamma': gamma, 'beta': beta, 'w_qkv': w_qkv}
    _L0_attn_in = _L0_attn_setup()

    def _L0_ffn_setup():
        import jax, jax.numpy as jnp
        import numpy as np
        import math
        DIM = 128
        H = 16
        HKV = 4
        HD = DIM // H
        MLP_MULT = 4
        HID = MLP_MULT * DIM
        BLK = 64
        BANK = 8
        TOPK = 2
        BASE = 10000.0
        B = 2
        T = 256
        EPS = 1e-06
        NEG = -1e+30

        def rms_norm(x):
            return x * jax.lax.rsqrt(jnp.mean(jnp.square(x), axis=-1, keepdims=True) + EPS)

        def blockdiag(x, w, nblocks):
            sh = x.shape[:-1]
            xr = x.reshape(-1, nblocks, BLK)
            wr = w.reshape(nblocks, BLK, BLK)
            return jnp.einsum('ngc,gcd->ngd', xr, wr).reshape(sh + (-1,))

        def bank_linear(x, s1, s2, mixw, logits):
            in_f = s1.shape[1]
            out_f = s2.shape[1]
            n_in = in_f // BLK
            n_out = out_f // BLK
            vals, idxs = jax.lax.top_k(logits, TOPK)
            coeffs = jax.nn.softmax(vals).astype(x.dtype)
            sh = x.shape[:-1]

            def member(w1, w2, wm, shift):
                h = blockdiag(x, w1, n_in)
                h3 = h.reshape(-1, n_in, BLK)
                h3 = jnp.roll(h3, shift, axis=1)
                h = jnp.swapaxes(h3, 1, 2).reshape(sh + (in_f,))
                h = h @ wm.T
                return blockdiag(h, w2, n_out)
            outs = jax.vmap(member)(s1[idxs], s2[idxs], mixw[idxs], idxs % n_in)
            return jnp.einsum('k,k...->...', coeffs, outs)

        def rope(x):
            t = jnp.arange(x.shape[2], dtype=jnp.float32)
            inv = 1.0 / BASE ** (jnp.arange(0, HD, 2, dtype=jnp.float32) / HD)
            fr = jnp.outer(t, inv)
            cos = jnp.cos(fr)[None, None]
            sin = jnp.sin(fr)[None, None]
            x1, x2 = (x[..., :HD // 2], x[..., HD // 2:])
            return jnp.concatenate([x1 * cos + x2 * sin, -x1 * sin + x2 * cos], axis=-1)

        def attention(x, wq, wk, wv, wo, q_gain, k_gain):
            Bt, Tt, _ = x.shape
            q = (x @ wq.T).reshape(Bt, Tt, H, HD).transpose(0, 2, 1, 3)
            k = (x @ wk.T).reshape(Bt, Tt, HKV, HD).transpose(0, 2, 1, 3)
            v = (x @ wv.T).reshape(Bt, Tt, HKV, HD).transpose(0, 2, 1, 3)
            q = rms_norm(q) * q_gain[None, :, None, None]
            k = rms_norm(k) * k_gain[None, :, None, None]
            q = rope(q)
            k = rope(k)
            rep = H // HKV
            k = jnp.repeat(k, rep, axis=1)
            v = jnp.repeat(v, rep, axis=1)
            scores = jnp.einsum('bhqd,bhkd->bhqk', q, k) / math.sqrt(HD)
            mask = jnp.tril(jnp.ones((Tt, Tt), bool))
            att = jax.nn.softmax(jnp.where(mask, scores, NEG), axis=-1)
            y = jnp.einsum('bhqk,bhkd->bhqd', att, v)
            return y.transpose(0, 2, 1, 3).reshape(Bt, Tt, DIM) @ wo.T
        key = jax.random.key(seed)
        ks = jax.random.split(key, 14)
        bound = 1.0 / math.sqrt(BLK)
        rn = lambda k, s, std: jax.random.normal(k, s, jnp.float32) * std
        un = lambda k, s: jax.random.uniform(k, s, jnp.float32, -bound, bound)
        return {'x': rn(ks[0], (B, T, DIM), 1.0), 'wq': rn(ks[1], (DIM, DIM), DIM ** (-0.5)), 'wk': rn(ks[2], (HKV * HD, DIM), DIM ** (-0.5)), 'wv': rn(ks[3], (HKV * HD, DIM), DIM ** (-0.5)), 'wo': rn(ks[4], (DIM, DIM), DIM ** (-0.5)), 'q_gain': jnp.ones((H,), jnp.float32), 'k_gain': jnp.ones((HKV,), jnp.float32), 'fc_s1': un(ks[5], (BANK, DIM, BLK)), 'fc_s2': un(ks[6], (BANK, HID, BLK)), 'fc_mix': rn(ks[7], (BANK, HID, DIM), DIM ** (-0.5)), 'fc_logits': rn(ks[8], (BANK,), 0.1), 'pj_s1': un(ks[9], (BANK, HID, BLK)), 'pj_s2': un(ks[10], (BANK, DIM, BLK)), 'pj_mix': rn(ks[11], (BANK, DIM, HID), HID ** (-0.5)), 'pj_logits': rn(ks[12], (BANK,), 0.1)}
    _L0_ffn_in = _L0_ffn_setup()
    _d = {'L0_attn_x': _L0_attn_in['x'], 'L0_attn_gamma': _L0_attn_in['gamma'], 'L0_attn_beta': _L0_attn_in['beta'], 'L0_attn_w_qkv': _L0_attn_in['w_qkv'], 'L0_ffn_wq': _L0_ffn_in['wq'], 'L0_ffn_wk': _L0_ffn_in['wk'], 'L0_ffn_wv': _L0_ffn_in['wv'], 'L0_ffn_wo': _L0_ffn_in['wo'], 'L0_ffn_q_gain': _L0_ffn_in['q_gain'], 'L0_ffn_k_gain': _L0_ffn_in['k_gain'], 'L0_ffn_fc_s1': _L0_ffn_in['fc_s1'], 'L0_ffn_fc_s2': _L0_ffn_in['fc_s2'], 'L0_ffn_fc_mix': _L0_ffn_in['fc_mix'], 'L0_ffn_fc_logits': _L0_ffn_in['fc_logits'], 'L0_ffn_pj_s1': _L0_ffn_in['pj_s1'], 'L0_ffn_pj_s2': _L0_ffn_in['pj_s2'], 'L0_ffn_pj_mix': _L0_ffn_in['pj_mix'], 'L0_ffn_pj_logits': _L0_ffn_in['pj_logits']}
    _x0 = _d['L0_attn_x']
    _d['L0_attn_x'] = jax.random.normal(jax.random.fold_in(jax.random.key(seed), 1), (8, 256, 128), dtype=_x0.dtype)
    del _x0
    return _d

def reference(L0_attn_x, L0_attn_gamma, L0_attn_beta, L0_attn_w_qkv, L0_ffn_wq, L0_ffn_wk, L0_ffn_wv, L0_ffn_wo, L0_ffn_q_gain, L0_ffn_k_gain, L0_ffn_fc_s1, L0_ffn_fc_s2, L0_ffn_fc_mix, L0_ffn_fc_logits, L0_ffn_pj_s1, L0_ffn_pj_s2, L0_ffn_pj_mix, L0_ffn_pj_logits):

    def _L0_attn_ref(x, gamma, beta, w_qkv):
        import jax, jax.numpy as jnp
        import numpy as np
        B, N, E, H = (2, 256, 128, 16)
        D = E // H
        LN_EPS = 1e-05
        b, n, e = x.shape
        h, d = (H, E // H)
        mu = jnp.mean(x, axis=-1, keepdims=True)
        var = jnp.mean(jnp.square(x - mu), axis=-1, keepdims=True)
        xn = (x - mu) * jax.lax.rsqrt(var + LN_EPS) * gamma + beta
        qkv = jnp.einsum('bne,fe->bnf', xn, w_qkv)
        q, k, v = jnp.split(qkv, 3, axis=-1)

        def to_heads(t):
            return t.reshape(b, n, h, d).transpose(0, 2, 1, 3)
        q = to_heads(q) * d ** (-0.5)
        k = to_heads(k)
        v = to_heads(v)
        sim = jnp.einsum('bhqd,bhkd->bhqk', q, k)
        causal_mask = jnp.triu(jnp.ones((n, n), dtype=bool), k=1)
        neg = -jnp.finfo(sim.dtype).max
        sim = jnp.where(causal_mask, neg, sim)
        attn = jax.nn.softmax(sim, axis=-1)
        out = jnp.einsum('bhqk,bhkd->bhqd', attn, v)
        return out.transpose(0, 2, 1, 3).reshape(b, n, h * d)

    def _L0_ffn_ref(x, wq, wk, wv, wo, q_gain, k_gain, fc_s1, fc_s2, fc_mix, fc_logits, pj_s1, pj_s2, pj_mix, pj_logits):
        import jax, jax.numpy as jnp
        import numpy as np
        import math
        DIM = 128
        H = 16
        HKV = 4
        HD = DIM // H
        MLP_MULT = 4
        HID = MLP_MULT * DIM
        BLK = 64
        BANK = 8
        TOPK = 2
        BASE = 10000.0
        B = 2
        T = 256
        EPS = 1e-06
        NEG = -1e+30

        def rms_norm(x):
            return x * jax.lax.rsqrt(jnp.mean(jnp.square(x), axis=-1, keepdims=True) + EPS)

        def blockdiag(x, w, nblocks):
            sh = x.shape[:-1]
            xr = x.reshape(-1, nblocks, BLK)
            wr = w.reshape(nblocks, BLK, BLK)
            return jnp.einsum('ngc,gcd->ngd', xr, wr).reshape(sh + (-1,))

        def bank_linear(x, s1, s2, mixw, logits):
            in_f = s1.shape[1]
            out_f = s2.shape[1]
            n_in = in_f // BLK
            n_out = out_f // BLK
            vals, idxs = jax.lax.top_k(logits, TOPK)
            coeffs = jax.nn.softmax(vals).astype(x.dtype)
            sh = x.shape[:-1]

            def member(w1, w2, wm, shift):
                h = blockdiag(x, w1, n_in)
                h3 = h.reshape(-1, n_in, BLK)
                h3 = jnp.roll(h3, shift, axis=1)
                h = jnp.swapaxes(h3, 1, 2).reshape(sh + (in_f,))
                h = h @ wm.T
                return blockdiag(h, w2, n_out)
            outs = jax.vmap(member)(s1[idxs], s2[idxs], mixw[idxs], idxs % n_in)
            return jnp.einsum('k,k...->...', coeffs, outs)

        def rope(x):
            t = jnp.arange(x.shape[2], dtype=jnp.float32)
            inv = 1.0 / BASE ** (jnp.arange(0, HD, 2, dtype=jnp.float32) / HD)
            fr = jnp.outer(t, inv)
            cos = jnp.cos(fr)[None, None]
            sin = jnp.sin(fr)[None, None]
            x1, x2 = (x[..., :HD // 2], x[..., HD // 2:])
            return jnp.concatenate([x1 * cos + x2 * sin, -x1 * sin + x2 * cos], axis=-1)

        def attention(x, wq, wk, wv, wo, q_gain, k_gain):
            Bt, Tt, _ = x.shape
            q = (x @ wq.T).reshape(Bt, Tt, H, HD).transpose(0, 2, 1, 3)
            k = (x @ wk.T).reshape(Bt, Tt, HKV, HD).transpose(0, 2, 1, 3)
            v = (x @ wv.T).reshape(Bt, Tt, HKV, HD).transpose(0, 2, 1, 3)
            q = rms_norm(q) * q_gain[None, :, None, None]
            k = rms_norm(k) * k_gain[None, :, None, None]
            q = rope(q)
            k = rope(k)
            rep = H // HKV
            k = jnp.repeat(k, rep, axis=1)
            v = jnp.repeat(v, rep, axis=1)
            scores = jnp.einsum('bhqd,bhkd->bhqk', q, k) / math.sqrt(HD)
            mask = jnp.tril(jnp.ones((Tt, Tt), bool))
            att = jax.nn.softmax(jnp.where(mask, scores, NEG), axis=-1)
            y = jnp.einsum('bhqk,bhkd->bhqd', att, v)
            return y.transpose(0, 2, 1, 3).reshape(Bt, Tt, DIM) @ wo.T
        x = x + attention(rms_norm(x), wq, wk, wv, wo, q_gain, k_gain)
        h = rms_norm(x)
        h = jnp.square(jax.nn.relu(bank_linear(h, fc_s1, fc_s2, fc_mix, fc_logits)))
        x = x + bank_linear(h, pj_s1, pj_s2, pj_mix, pj_logits)
        return x
    x = L0_attn_x
    x = _layernorm(x + _L0_attn_ref(x, L0_attn_gamma, L0_attn_beta, L0_attn_w_qkv), axis=-1)
    x = _layernorm(x + _L0_ffn_ref(x, L0_ffn_wq, L0_ffn_wk, L0_ffn_wv, L0_ffn_wo, L0_ffn_q_gain, L0_ffn_k_gain, L0_ffn_fc_s1, L0_ffn_fc_s2, L0_ffn_fc_mix, L0_ffn_fc_logits, L0_ffn_pj_s1, L0_ffn_pj_s2, L0_ffn_pj_mix, L0_ffn_pj_logits), axis=-1)
    return x

_drawn_inputs = setup_inputs


def setup_inputs(seed=0):
    import zlib

    import numpy as np

    out = dict(_drawn_inputs(seed))
    spreads = {'L0_attn_gamma': (1.0, 0.2),
     'L0_attn_beta': (0.0, 0.1),
     'L0_ffn_q_gain': (1.0, 0.6),
     'L0_ffn_k_gain': (1.0, 0.6)}
    factors = {'L0_ffn_fc_s1': 7.679,
     'L0_ffn_fc_s2': 7.753,
     'L0_ffn_fc_mix': 7.741,
     'L0_ffn_fc_logits': 7.623,
     'L0_ffn_pj_s1': 7.017,
     'L0_ffn_pj_s2': 6.982,
     'L0_ffn_pj_mix': 6.963,
     'L0_ffn_pj_logits': 7.064}
    for name, (base, spread) in spreads.items():
        noise = np.random.default_rng([zlib.crc32(name.encode()), seed]).standard_normal(out[name].shape)
        drawn = base * np.exp(spread * noise) if base else spread * noise
        out[name] = jnp.asarray(drawn.astype(out[name].dtype))
    for name, factor in factors.items():
        out[name] = (out[name] * factor).astype(out[name].dtype)
    return out
```

```python
from contextlib import ExitStack

import concourse.bass as bass
from concourse import mybir

F32 = mybir.dt.float32
BF16 = mybir.dt.bfloat16
U32 = mybir.dt.uint32
ALU = mybir.AluOpType
ACT = mybir.ActivationFunctionType
AX_X = mybir.AxisListType.X

P = 128
BATCH, SEQ, E = 8, 256, 128
HEADS, KV_HEADS, D = 16, 4, 8
GROUPS, QUADS = 4, 4
STRIP = 32
STRIPS = SEQ // STRIP
PAIR = 2
TOK = PAIR * SEQ
TILES = TOK // P
ROWS = 3 * STRIP
MROWS = ROWS + QUADS
HID, BLK, BANK, TOPK = 512, 64, 8, 2
NB_IN = {"fc": E // BLK, "pj": HID // BLK}
SCALE = float(D) ** -0.5
LN_EPS, RMS_EPS = 1e-5, 1e-6

CONSTS = {}
_at = 0
for _name, _width in (("ident", P), ("perm", P), ("mask_s", STRIP), ("mask_st", STRIP), ("quad", QUADS),
                      ("ones_bd", STRIP), ("negsel", P), ("cos", TILES * D), ("sin", TILES * D), ("ones", BLK)):
    CONSTS[_name] = (_at, _at + _width)
    _at += _width
CONST_COLS = _at


def score_units():
    units = []
    for s in (7, 6, 5, 4):
        units += [[(s, 0, 2, 0)], [(s, 2, 2, 0)]]
    units += [[(3, 0, 4, 0)], [(2, 0, 4, 0)], [(1, 0, 4, 0), (0, 0, 4, 256)]]
    return units


def prob_units():
    units = []
    for a, b in ((0, None), (1, 7), (2, 6), (3, 5)):
        for g in (0, 2):
            unit = [(a, g, 2, 0)]
            if b is not None:
                unit.append((b, g, 2, 2 * (SEQ - STRIP * a)))
            units.append(unit)
    units.append([(4, 0, 4, 0)])
    return units


S_UNITS, P_UNITS = score_units(), prob_units()
NS, NP = len(S_UNITS), len(P_UNITS)
S_RING, T_RING, P_RING = 2, 3, 4
N_REDUCE = sum(len(u) for u in S_UNITS)


def keys_of(s):
    return STRIP * (s + 1)


def queries_of(s):
    return SEQ - STRIP * s


def build(nc, io, out):
    with ExitStack() as ctx:
        def sb(name, shape, dt=F32):
            return ctx.enter_context(nc.sbuf_tensor(name, shape, dt))

        def psum(name, shape, dt=F32):
            return ctx.enter_context(nc.psum_tensor(name, shape, dt))

        def sem(name):
            return ctx.enter_context(nc.semaphore(name))

        front = psum("front", [P, 2, 512])
        score = psum("score", [P, S_RING, 512])
        score_t = psum("score_t", [P, T_RING, 512])
        pv_bank = psum("pv_bank", [P, 512])

        cst = sb("cst", [P, CONST_COLS])

        def const(name):
            return cst[:, CONSTS[name][0]:CONSTS[name][1]]

        setup_ctx = ExitStack()

        def ts(name, shape, dt=F32):
            return setup_ctx.enter_context(nc.sbuf_tensor(name, shape, dt))

        ident_b = sb("ident_b", [P, P], BF16)
        mask_s = sb("mask_s", [P, STRIP], BF16)
        mask_st = sb("mask_st", [P, STRIP], BF16)
        negsel = sb("negsel", [P, P], BF16)
        gamma = sb("gamma", [P, 1])
        beta = sb("beta", [P, 1])
        gain = sb("gain", [P, TILES * (HEADS + KV_HEADS)])
        cos_q, sin_q = sb("cos_q", [P, TOK]), sb("sin_q", [P, TOK])
        cos_k, sin_k = sb("cos_k", [P, P]), sb("sin_k", [P, P])
        wq_t, wk_t = sb("wq_t", [P, P]), sb("wk_t", [P, P])
        wv_t = [sb(f"wv_t{l}", [P, P]) for l in range(2)]
        wqk_t = sb("wqk_t", [P, P + KV_HEADS * D])
        wo_t = sb("wo_t", [P, P])

        w_fc = sb("w_fc", [P, HID])
        w_pj = sb("w_pj", [P, 4, P])

        minus_half = sb("minus_half", [P, TILES])
        k_bd = [sb(f"k_bd{n}", [MROWS, GROUPS * TOK // STRIP, P], BF16) for n in range(2)]
        v_bd = sb("v_bd", [P, PAIR * STRIPS, GROUPS, STRIP])

        gain_in = ts("gain_in", [P, HEADS + KV_HEADS])
        w_raw = ts("w_raw", [P, 5, P])
        wkv_raw = ts("wkv_raw", [2 * KV_HEADS * D, P])
        wo_perm = ts("wo_perm", [P, P])
        logits = ts("logits", [1, 2, BANK])
        top_v = ts("top_v", [1, 2, 8])
        top_i = ts("top_i", [1, 2, 8], U32)
        coef = ts("coef", [1, 2, TOPK])
        coef_tmp = ts("coef_tmp", [1, 3, 2])
        coef_b = ts("coef_b", [BLK, 2 * TOPK])
        fc_mix_sb = [ts(f"fc_mix_sb{k}", [P, 4, P]) for k in range(TOPK)]
        fc_s2_sb = [ts(f"fc_s2_sb{k}", [P, 4, BLK]) for k in range(TOPK)]
        fc_s1_sb = [ts(f"fc_s1_sb{k}", [P, BLK]) for k in range(TOPK)]
        pj_mix_sb = [ts(f"pj_mix_sb{k}", [P, HID]) for k in range(TOPK)]
        pj_s2_sb = [ts(f"pj_s2_sb{k}", [P, BLK]) for k in range(TOPK)]
        pj_s1_sb = [ts(f"pj_s1_sb{k}", [P, 4, BLK]) for k in range(TOPK)]
        fc_s1_t = [ts(f"fc_s1_t{k}", [BLK, P]) for k in range(TOPK)]
        pj_s1_t = [ts(f"pj_s1_t{k}", [BLK, HID]) for k in range(TOPK)]
        twice = [ts(f"twice{m}", [BLK, 2, 1024]) for m in range(4)]
        rolled = [ts(f"rolled{m}", [BLK, 1024]) for m in range(4)]

        cst_in, w_in, small_in, logit_in, bank_in = (sem(n) for n in ("cst_in", "w_in", "small_in", "logit_in", "bank_in"))
        top_done, exp_done, coef_done, coefp_done, coefb_done = (sem(n) for n in ("top_done", "exp_done", "coef_done", "coefp_done", "coefb_done"))
        wo_ready, w_tr, w_ready, b16_ready, neg_in = (sem(n) for n in ("wo_ready", "w_tr", "w_ready", "b16_ready", "neg_in"))
        s1_tr, s1_ready, mixed, mix_read, roll_in, folded, fold_read = (sem(n) for n in ("s1_tr", "s1_ready", "mixed", "mix_read", "roll_in", "folded", "fold_read"))
        pool_set, set_chain = sem("pool_set"), sem("set_chain")

        with nc.Block() as block:
            @block.sync
            def _(sp):
                sp.dma_start(logits[:, 0, :], io["fc_logits"].rearrange("(a b) -> a b", a=1)).then_inc(logit_in, 16)
                sp.dma_start(logits[:, 1, :], io["pj_logits"].rearrange("(a b) -> a b", a=1)).then_inc(logit_in, 16)
                sp.dma_start(cst[:], io["consts"]).then_inc(cst_in, 16)
                sp.dma_start(w_raw[:, 0:3, :], io["w_qkv"].rearrange("(s p) e -> p s e", p=P)).then_inc(w_in, 16)
                sp.dma_start(w_raw[:, 3, :], io["wq"]).then_inc(w_in, 16)
                sp.dma_start(w_raw[:, 4, :], io["wo"]).then_inc(w_in, 16)
                sp.dma_start(wkv_raw[0:32, :], io["wk"]).then_inc(w_in, 16)
                sp.dma_start(wkv_raw[32:64, :], io["wv"]).then_inc(w_in, 16)
                sp.dma_start(gamma[:], io["gamma"].rearrange("(a b) -> a b", b=1)).then_inc(small_in, 16)
                sp.dma_start(beta[:], io["beta"].rearrange("(a b) -> a b", b=1)).then_inc(small_in, 16)
                sp.dma_start(gain_in[:, 0:HEADS], io["q_gain"].partition_broadcast(P)).then_inc(small_in, 16)
                sp.dma_start(gain_in[:, HEADS:], io["k_gain"].partition_broadcast(P)).then_inc(small_in, 16)
                sp.wait_ge(top_done, 2)
                member = []
                for w, kind in enumerate(("fc", "pj")):
                    for k in range(TOPK):
                        idx = sp.value_load(top_i[0:1, w, k:k + 1], min_val=0, max_val=BANK - 1)
                        member.append(idx)
                        if kind == "fc":
                            mix, s2, s1 = fc_mix_sb[k][:], fc_s2_sb[k][:], fc_s1_sb[k][:]
                            mix_d = io["fc_mix"].rearrange("a b c -> (a b) c")[bass.ds(idx * HID, HID)].rearrange("(t p) c -> p t c", p=P)
                            s2_d = io["fc_s2"].rearrange("a b c -> (a b) c")[bass.ds(idx * HID, HID)].rearrange("(t p) c -> p t c", p=P)
                            s1_d = io["fc_s1"].rearrange("a b c -> (a b) c")[bass.ds(idx * E, E)]
                        else:
                            mix, s2, s1 = pj_mix_sb[k][:], pj_s2_sb[k][:], pj_s1_sb[k][:]
                            mix_d = io["pj_mix"].rearrange("a b c -> (a b) c")[bass.ds(idx * E, E)]
                            s2_d = io["pj_s2"].rearrange("a b c -> (a b) c")[bass.ds(idx * E, E)]
                            s1_d = io["pj_s1"].rearrange("a b c -> (a b) c")[bass.ds(idx * HID, HID)].rearrange("(t p) c -> p t c", p=P)
                        sp.dma_start(mix, mix_d).then_inc(bank_in, 16)
                        sp.dma_start(s2, s2_d).then_inc(bank_in, 16)
                        sp.dma_start(s1, s1_d).then_inc(bank_in, 16)
                sp.wait_ge(b16_ready, 1)
                for n in range(2):
                    src = negsel[ROWS:MROWS, :].rearrange("p (o n) -> p o n", o=1).to_broadcast([QUADS, GROUPS * TOK // STRIP, P])
                    sp.dma_start(k_bd[n][ROWS:MROWS, :, :], src).then_inc(neg_in, 16)
                for m in range(4):
                    sp.wait_ge(mix_read, 4 * (m + 1))
                    n_in = NB_IN["fc"] if m < 2 else NB_IN["pj"]
                    shift = (member[m] % n_in) * (1024 // n_in)
                    flat = twice[m][:].rearrange("p a n -> p (a n)")
                    sp.dma_start(rolled[m][:], flat[:, bass.ds(shift, 1024)]).then_inc(roll_in, 16)
                sp.wait_ge(neg_in, 32)

            @block.gpsimd
            def _(pool):
                nc.gpsimd.memset(minus_half[:], -0.5)
                nc.gpsimd.memset(v_bd[:], 0.0).then_inc(pool_set, 1)
                pool.wait_ge(pool_set, 1)

            @block.scalar
            def _(act):
                act.wait_ge(coef_done, 1)
                nc.scalar.activation(coef_tmp[:, 1, :], coef_tmp[:, 0, :], ACT.Exp).then_inc(exp_done, 1)
                act.wait_ge(coefb_done, 1)
                for m in range(4):
                    act.wait_ge(mixed, m + 1)
                    w, k = divmod(m, TOPK)
                    for half in range(2):
                        src = score[0:BLK, half, :]
                        for rep in range(2):
                            if w == 0:
                                dst = twice[m][:, rep, :].rearrange("p (g t h e) -> p g t h e", g=2, t=4, h=2)[:, :, :, half, :]
                                s4 = src.rearrange("p (g t e) -> p g t e", g=2, t=4)
                            else:
                                dst = twice[m][:, rep, :].rearrange("p (g h e) -> p g h e", g=8, h=2)[:, :, half, :]
                                s4 = src.rearrange("p (g e) -> p g e", g=8)
                            nc.scalar.activation(dst, s4, ACT.Copy, scale=coef_b[:, m:m + 1]).then_inc(mix_read, 1)

            @block.vector
            def _(dve):
                n_chain = [0]

                def link(ins):
                    n_chain[0] += 1
                    ins.then_inc(set_chain, 1)
                    dve.wait_ge(set_chain, n_chain[0])

                dve.wait_ge(logit_in, 32)
                for w in range(2):
                    nc.vector.max(top_v[:, w, :], logits[:, w, :]).then_inc(set_chain, 1)
                    n_chain[0] += 1
                dve.wait_ge(set_chain, n_chain[0])
                for w in range(2):
                    nc.vector.max_index(top_i[:, w, :], top_v[:, w, :], logits[:, w, :]).then_inc(top_done, 1)
                nc.vector.tensor_tensor(coef_tmp[:, 0, :], top_v[:, :, 1], top_v[:, :, 0], ALU.subtract).then_inc(coef_done, 1)
                dve.wait_ge(exp_done, 1)
                link(nc.vector.tensor_scalar(coef_tmp[:, 2, :], coef_tmp[:, 1, :], 1.0, None, ALU.add))
                link(nc.vector.reciprocal(coef[:, :, 0], coef_tmp[:, 2, :]))
                nc.vector.tensor_tensor(coef[:, :, 1], coef[:, :, 0], coef_tmp[:, 1, :], ALU.mult).then_inc(coef_done, 1)
                dve.wait_ge(cst_in, 16)
                nc.vector.tensor_copy(ident_b[:], const("ident"))
                nc.vector.tensor_copy(mask_s[:], const("mask_s"))
                nc.vector.tensor_copy(mask_st[:], const("mask_st"))
                nc.vector.tensor_copy(negsel[:], const("negsel")).then_inc(b16_ready, 1)
                dve.wait_ge(w_in, 80)
                nc.vector.tensor_copy(wo_perm[:].rearrange("p (g j c) -> p j g c", g=4, j=4),
                                      w_raw[:, 4, :].rearrange("p (j g c) -> p j g c", j=4, g=4)).then_inc(wo_ready, 1)
                dve.wait_ge(small_in, 64)
                for name, full_q, full_k in (("cos", cos_q, cos_k), ("sin", sin_q, sin_k)):
                    for t in range(TILES):
                        one = const(name)[:, t * D:(t + 1) * D].rearrange("p (o c) -> p o c", o=1)
                        nc.vector.tensor_copy(full_q[:, t * P:(t + 1) * P].rearrange("p (h c) -> p h c", c=D),
                                              one.to_broadcast([P, HEADS, D]))
                        nc.vector.tensor_copy(full_k[:, t * 32:(t + 1) * 32].rearrange("p (h c) -> p h c", c=D),
                                              one.to_broadcast([P, KV_HEADS, D]))
                nc.vector.tensor_copy(gain[:, 0:64].rearrange("p (t h) -> p t h", t=TILES),
                                      gain_in[:, 0:HEADS].rearrange("p (o h) -> p o h", o=1).to_broadcast([P, TILES, HEADS]))
                nc.vector.tensor_copy(gain[:, 64:80].rearrange("p (t h) -> p t h", t=TILES),
                                      gain_in[:, HEADS:].rearrange("p (o h) -> p o h", o=1).to_broadcast([P, TILES, KV_HEADS]))
                dve.wait_ge(w_tr, 1)
                tr = front[:, 0, :].rearrange("p (s n) -> p s n", s=4)
                for w, dst in ((0, wq_t), (1, wk_t)):
                    nc.vector.tensor_copy(dst[:].rearrange("p (j c g) -> p j g c", j=4, c=D),
                                          tr[:, w, :].rearrange("p (j g c) -> p j g c", j=4, g=4))
                nc.vector.tensor_copy(wv_t[0][:], tr[:, 2, :])
                nc.vector.tensor_copy(wqk_t[:, 0:P], tr[:, 3, :])
                nc.vector.tensor_copy(wqk_t[:, P:P + 32], front[:, 1, 0:32])
                for g in range(GROUPS):
                    nc.vector.tensor_copy(wv_t[1][:].rearrange("p (j g c) -> p j g c", j=4, g=4)[:, :, g, :],
                                          front[:, 1, 32:64].rearrange("p (j c) -> p j c", j=4))
                nc.vector.tensor_copy(wo_t[:], front[:, 1, 128:256]).then_inc(w_ready, 1)
                dve.wait_ge(s1_tr, 1)
                for k in range(TOPK):
                    nc.vector.tensor_copy(fc_s1_t[k][:], pv_bank[0:BLK, k * P:(k + 1) * P])
                    nc.vector.tensor_copy(pj_s1_t[k][:], score_t[0:BLK, k, :])
                nc.vector.drain().then_inc(s1_ready, 1)
                dve.wait_ge(coefp_done, 1)
                nc.vector.tensor_copy(coef_b[:], score_t[0:BLK, 2, 0:4]).then_inc(coefb_done, 1)
                dve.wait_ge(folded, 1)
                nc.vector.tensor_copy(w_fc[:], front[:, 0, :])
                nc.vector.tensor_copy(w_pj[:].rearrange("p t n -> p (t n)"), front[:, 1, :]).then_inc(fold_read, 1)
                dve.wait_ge(fold_read, 1)

            @block.tensor
            def _(pe):
                pe.wait_ge(cst_in, 16)
                ident = const("ident")
                pe.wait_ge(coef_done, 2)
                pe.matmul(score_t[0:BLK, 2, 0:4], const("ones")[0:1, :], coef[:].rearrange("p a b -> p (a b)"),
                          start=True, stop=True).then_inc(coefp_done, 1)
                pe.wait_ge(w_in, 80)
                for s in range(4):
                    pe.transpose(front[:, 0, s * P:(s + 1) * P], w_raw[:, s, :], ident)
                pe.transpose(front[:, 1, 0:64], wkv_raw[:], ident[0:64, 0:64])
                pe.wait_ge(wo_ready, 1)
                pe.transpose(front[:, 1, 128:256], wo_perm[:], ident).then_inc(w_tr, 1)
                pe.wait_ge(bank_in, 16 * 12)
                for k in range(TOPK):
                    pe.transpose(pv_bank[0:BLK, k * P:(k + 1) * P], fc_s1_sb[k][:], ident)
                    for t in range(4):
                        mm = pe.transpose(score_t[0:BLK, k, t * P:(t + 1) * P], pj_s1_sb[k][:, t, :], ident)
                mm.then_inc(s1_tr, 1)
                for m in range(4):
                    w, k = divmod(m, TOPK)
                    if m:
                        pe.wait_ge(mix_read, 4 * m)
                    for half in range(2):
                        rows = slice(BLK * half, BLK * half + BLK)
                        for g in range(NB_IN["fc"] if w == 0 else NB_IN["pj"]):
                            if w == 0:
                                for t in range(4):
                                    mm = pe.matmul(score[0:BLK, half, (g * 4 + t) * BLK:(g * 4 + t + 1) * BLK],
                                                   fc_mix_sb[k][rows, t, :].rearrange("p (d g) -> p g d", g=2)[:, g, :],
                                                   fc_s2_sb[k][rows, t, :], start=True, stop=True)
                            else:
                                mm = pe.matmul(score[0:BLK, half, g * BLK:(g + 1) * BLK],
                                               pj_mix_sb[k][rows, :].rearrange("p (d g) -> p g d", g=8)[:, g, :],
                                               pj_s2_sb[k][rows, :], start=True, stop=True)
                    mm.then_inc(mixed, 1)
                pe.wait_ge(s1_ready, 1)
                pe.wait_ge(w_ready, 1)
                pe.wait_ge(roll_in, 64)
                for k in range(TOPK):
                    for g in range(2):
                        pe.matmul(front[BLK * g:BLK * g + BLK, 0, :], fc_s1_t[k][:, BLK * g:BLK * g + BLK],
                                  rolled[k][:, g * 512:(g + 1) * 512], start=(k == 0), stop=(k == 1), skip_group_check=True)
                for k in range(TOPK):
                    for g in range(8):
                        t, h = divmod(g, 2)
                        mm = pe.matmul(front[BLK * h:BLK * h + BLK, 1, t * P:(t + 1) * P],
                                       pj_s1_t[k][:, BLK * g:BLK * g + BLK], rolled[2 + k][:, g * P:(g + 1) * P],
                                       start=(k == 0 and t == 0), stop=(k == 1), skip_group_check=True)
                mm.then_inc(folded, 1)

        setup_ctx.close()
        x_in = sb("x_in", [P, TILES, E])
        x_hat = sb("x_hat", [P, TILES, E])
        x1 = sb("x1", [P, TILES, E])
        y1 = sb("y1", [P, TILES, E])
        x2 = sb("x2", [P, TILES, E])
        x3 = sb("x3", [P, TILES, E])
        x_out = sb("x_out", [P, TILES, E])
        junk = sb("junk", [P, E])
        bn = sb("bn", [P, TILES, 6])
        mv = sb("mv", [P, TILES, 2])
        var_eps = sb("var_eps", [P, TILES])
        sumsq = sb("sumsq", [P, TILES])
        rstd = sb("rstd", [P, TILES])
        x_t = [sb(f"x_t{n}", [P, TOK]) for n in range(3)]
        sq = sb("sq", [P, 5 * P])
        head_ss = sb("head_ss", [P, TILES * 20])
        head_rt = sb("head_rt", [P, TILES * 20])
        head_rr = sb("head_rr", [P, TILES * 20])
        head_rg = sb("head_rg", [P, TILES * 20])
        qn, kn = sb("qn", [P, TOK]), sb("kn", [P, P])
        qc, kc = sb("qc", [P, TOK]), sb("kc", [P, P])
        qs, ks = sb("qs", [P, TOK]), sb("ks", [P, P])
        q_rot, k_rot = sb("q_rot", [P, TOK]), sb("k_rot", [P, TOK])
        q_res, k_res = sb("q_res", [P, TOK]), sb("k_res", [P, TOK])
        q_parts, k_parts = sb("q_parts", [P, 3, TOK], BF16), sb("k_parts", [P, 3, TOK], BF16)
        q_rows = sb("q_rows", [MROWS, 2, GROUPS, TOK], BF16)
        k_rows = sb("k_rows", [ROWS, 2, GROUPS, TOK], BF16)
        q_bd = sb("q_bd", [ROWS, GROUPS * TOK // STRIP, P], BF16)
        mx = sb("mx", [P, PAIR, GROUPS, STRIPS])
        mx_parts = sb("mx_parts", [P, PAIR, 2, GROUPS * STRIPS], BF16)
        mx_t = sb("mx_t", [2 * GROUPS * STRIPS, PAIR, P], BF16)
        probs = sb("probs", [P, P_RING, 512])
        rden = sb("rden", [P, SEQ])
        y_t = sb("y_t", [P, TOK])
        relu = sb("relu", [P, 2, TOK])
        hid_t = sb("hid_t", [P, 4, TOK])


        loop_sems = []

        def lsem(name):
            s = sem(name)
            loop_sems.append(s)
            return s

        x_loaded, x_stored = lsem("x_loaded"), lsem("x_stored")
        dve_order, act_order, pool_order = lsem("dve_order"), lsem("act_order"), lsem("pool_order")
        norm_in, norm_rstd, hat_ready, hat_t, xt_ready, sq_done = (lsem(n) for n in ("norm_in", "norm_rstd", "hat_ready", "hat_t", "xt_ready", "sq_done"))
        y_tr, wo_done, fc_done, relu_done, hid_ready, pj_done, out_ready = (lsem(n) for n in ("y_tr", "wo_done", "fc_done", "relu_done", "hid_ready", "pj_done", "out_ready"))
        tok_read = lsem("tok_read")
        proj_tok, head_sq, head_sum, head_root, rope_done, rope_tr, rope_mul, qk_high, qk_split = (lsem(n) for n in ("proj_tok", "head_sq", "head_sum", "head_root", "rope_done", "rope_tr", "rope_mul", "qk_high", "qk_split"))
        L = []
        for l in range(2):
            L.append({n: lsem(f"{n}{l}") for n in (
                "qk_proj", "v_proj", "v_ready", "high", "resid", "mid", "low", "rows_in", "bd_ready",
                "s_done", "s_read", "m_ready", "m_tr", "m_copied", "m_in", "t_done", "p_ready", "pv_done", "y_ready")})
        NPAIR = BATCH // PAIR

        with nc.Fori(0, NPAIR) as pair:
            x_rows = io["x"].rearrange("b n e -> (b n) e")[bass.ds(pair * TOK, TOK)].rearrange("(t p) e -> p t e", p=P)
            o_rows = out.rearrange("b n e -> (b n) e")[bass.ds(pair * TOK, TOK)].rearrange("(t p) e -> p t e", p=P)

            with nc.Block() as block:
                @block.sync
                def _(sp):
                    sp.dma_start(x_in[:], x_rows).then_inc(x_loaded, 16)
                    for l in range(2):
                        s = L[l]
                        for src, dst, parts in ((k_parts, k_rows, ((0, 1, 0), (0, 1, 2))), (q_parts, q_rows, ((0, 0, 1), (2, 1, 0)))):
                            for n in range(2):
                                for t in range(3):
                                    part = parts[n][t]
                                    sp.wait_ge(s[("high", "mid", "low")[part]], 1 if src is k_parts else 2)
                                    sp.dma_start(dst[32 * t:32 * t + 32, n, :, :], src[:, part, :]).then_inc(s["rows_in"], 16)
                        for b in range(PAIR):
                            sp.wait_ge(s["m_copied"], b + 1)
                            for j in range(QUADS):
                                sp.dma_start(q_rows[ROWS + j:ROWS + j + 1].rearrange("p a g (s b n) -> p (a g s) b n", b=PAIR, n=STRIP)[:, :, b, :],
                                             mx_t[:, b, STRIP * j:STRIP * j + STRIP]).then_inc(s["m_in"], 16)
                    sp.wait_ge(out_ready, 1)
                    sp.dma_start(o_rows, x_out[:]).then_inc(x_stored, 16)
                    sp.wait_ge(x_stored, 16)

                @block.gpsimd
                def _(pool):
                    def root(n):
                        pool.wait_ge(norm_in, n)
                        nc.gpsimd.tensor_tensor(rstd[:], var_eps[:], minus_half[:], ALU.pow).then_inc(norm_rstd, 1)

                    root(1)
                    root(2)
                    root(3)
                    pool.wait_ge(rope_mul, 2)
                    nc.gpsimd.tensor_tensor(q_rot[:].rearrange("p (a c g) -> p a g c", c=D, g=4),
                                            qc[:].rearrange("p (a g c) -> p a g c", g=4, c=D),
                                            qs[:].rearrange("p (a g c) -> p a g c", g=4, c=D), ALU.add).then_inc(rope_done, 1)
                    root(4)
                    root(5)

                @block.scalar
                def _(act):
                    def square_sums(n, src):
                        for t in range(TILES):
                            if t:
                                act.wait_ge(sq_done, (n - 1) * TILES + t)
                            nc.scalar.activation(junk[:], src[:, t, :], ACT.Square, accum_out=sumsq[:, t:t + 1]).then_inc(sq_done, 1)

                    def attention(l):
                        s = L[l]
                        act.wait_ge(s["v_proj"], 1)
                        for j in range(QUADS):
                            q = slice(32 * j, 32 * j + 32)
                            cp = nc.scalar.activation(v_bd[q, :, :, D * j:D * j + D],
                                                      pv_bank[q, :].rearrange("p (s g c) -> p s g c", g=4, c=D), ACT.Copy)
                        cp.then_inc(s["v_ready"], 1)
                        for n, (bank, parts, res) in enumerate(((1, k_parts, k_res), (0, q_parts, q_res))):
                            act.wait_ge(s["qk_proj"], n + 1)
                            nc.scalar.activation(parts[:, 0, :], front[:, bank, :], ACT.Copy).then_inc(s["high"], 1)
                        for n, (parts, res) in enumerate(((k_parts, k_res), (q_parts, q_res))):
                            act.wait_ge(s["resid"], n + 1)
                            nc.scalar.activation(parts[:, 1, :], res[:], ACT.Copy).then_inc(s["mid"], 1)
                        for n in range(PAIR * NP):
                            act.wait_ge(s["t_done"], n + 1)
                            if n >= P_RING:
                                b, u = divmod(n - P_RING, NP)
                                act.wait_ge(s["pv_done"], b * 5 + (u // 2) + 1)
                            nc.scalar.activation(probs[:, n % P_RING, :], score_t[:, n % T_RING, :], ACT.Exp,
                                                 scale=SCALE).then_inc(s["p_ready"], 1)

                    attention(0)
                    act.wait_ge(hat_ready, 2)
                    square_sums(1, y1)
                    act.wait_ge(hat_t, 2)
                    nc.scalar.activation(x_t[1][:], front[:, 0, :], ACT.Copy).then_inc(xt_ready, 1)
                    act.wait_ge(proj_tok, 1)
                    nc.scalar.activation(sq[:, 0:TOK].rearrange("p (b n) -> p b n", b=2), front[:, :, 0:256], ACT.Square)
                    nc.scalar.activation(sq[:, TOK:].rearrange("p (b n) -> p b n", b=2), front[:, :, 256:320], ACT.Square).then_inc(head_sq, 1)
                    act.wait_ge(head_sum, 1)
                    nc.scalar.activation(head_rt[:], head_ss[:], ACT.Sqrt).then_inc(head_root, 1)
                    attention(1)
                    act.wait_ge(tok_read, 2)
                    square_sums(2, x2)
                    act.wait_ge(hat_t, 3)
                    nc.scalar.activation(x_t[2][:], front[:, 1, :], ACT.Copy).then_inc(xt_ready, 1)
                    for h in range(4):
                        act.wait_ge(fc_done, h + 1)
                        if h >= 2:
                            act.wait_ge(hid_ready, h - 1)
                        nc.scalar.activation(relu[:, h % 2, :], score[:, h % 2, :], ACT.Relu).then_inc(relu_done, 1)

                @block.vector
                def _(dve):
                    n_order = [0]

                    def link(ins):
                        n_order[0] += 1
                        ins.then_inc(dve_order, 1)
                        dve.wait_ge(dve_order, n_order[0])

                    def last(ins):
                        link(ins)

                    def layer_norm(n, src, dst, stage):
                        for t in range(TILES):
                            ins = nc.vector.bn_stats(bn[:, t, :], src[:, t, :])
                        link(ins)
                        for t in range(TILES):
                            ins = nc.vector.bn_aggr(mv[:, t, :], bn[:, t, :])
                        link(ins)
                        nc.vector.tensor_scalar(var_eps[:], mv[:, :, 1], LN_EPS, None, ALU.add).then_inc(norm_in, 1)
                        dve.wait_ge(norm_rstd, n)
                        for t in range(TILES):
                            ins = nc.vector.tensor_scalar(dst[:, t, :], src[:, t, :], mv[:, t, 0:1], rstd[:, t:t + 1],
                                                          ALU.subtract, ALU.mult)
                        ins.then_inc(stage, 1)

                    def rms_norm(n, k, src, dst):
                        dve.wait_ge(sq_done, k * TILES)
                        nc.vector.tensor_scalar(var_eps[:], sumsq[:], 1.0 / E, RMS_EPS, ALU.mult, ALU.add).then_inc(norm_in, 1)
                        dve.wait_ge(norm_rstd, n)
                        for t in range(TILES):
                            ins = nc.vector.tensor_scalar(dst[:, t, :], src[:, t, :], rstd[:, t:t + 1], None, ALU.mult)
                        ins.then_inc(hat_ready, 1)

                    def attention(l):
                        s = L[l]
                        for n, (bank, parts, res) in enumerate(((1, k_parts, k_res), (0, q_parts, q_res))):
                            dve.wait_ge(s["high"], n + 1)
                            nc.vector.tensor_tensor(res[:], front[:, bank, :], parts[:, 0, :], ALU.subtract).then_inc(s["resid"], 1)
                        for n, (parts, res) in enumerate(((k_parts, k_res), (q_parts, q_res))):
                            dve.wait_ge(s["mid"], n + 1)
                            nc.vector.tensor_tensor(parts[:, 2, :], res[:], parts[:, 1, :], ALU.subtract).then_inc(s["low"], 1)
                        dve.wait_ge(s["rows_in"], 12 * 16)
                        quad = const("quad")
                        for src, dst in ((q_rows[0:ROWS, 0], q_bd), (k_rows[0:ROWS, 0], k_bd[0]), (k_rows[0:ROWS, 1], k_bd[1])):
                            for j in range(QUADS):
                                ins = nc.vector.tensor_scalar(dst[0:ROWS, :, STRIP * j:STRIP * j + STRIP],
                                                              src.rearrange("p g (s n) -> p (g s) n", n=STRIP),
                                                              quad[0:ROWS, j:j + 1], None, ALU.mult)
                            ins.then_inc(s["bd_ready"], 1)
                        for b in range(PAIR):
                            for u, unit in enumerate(S_UNITS):
                                n = b * NS + u
                                dve.wait_ge(s["s_done"], n + 1)
                                for strip, g0, ng, off in unit:
                                    w = keys_of(strip)
                                    ins = nc.vector.tensor_reduce(mx[:, b, g0:g0 + ng, strip],
                                                                  score[:, n % S_RING, off:off + ng * w].rearrange("p (g k) -> p g k", g=ng),
                                                                  AX_X, ALU.max)
                                ins.then_inc(s["s_read"], 1)
                            dve.wait_ge(s["s_read"], (b + 1) * NS)
                            flat = mx[:, b].rearrange("p g s -> p (g s)")
                            link(nc.vector.tensor_copy(mx_parts[:, b, 0, :], flat))
                            nc.vector.tensor_tensor(mx_parts[:, b, 1, :], flat, mx_parts[:, b, 0, :], ALU.subtract).then_inc(s["m_ready"], 1)
                            dve.wait_ge(s["m_tr"], b + 1)
                            nc.vector.tensor_copy(mx_t[:, b, :], front[0:64, 0, 0:64].bitcast(BF16)).then_inc(s["m_copied"], 1)
                        for b in range(PAIR):
                            bank = pv_bank[:, :] if b == 0 else front[:, 1, :]
                            dve.wait_ge(s["pv_done"], (b + 1) * 5)
                            if b:
                                dve.wait_ge(s["y_ready"], b)
                            link(nc.vector.reciprocal(rden[:], bank[:, SEQ:]))
                            nc.vector.tensor_tensor(y_t[:, b * SEQ:(b + 1) * SEQ], bank[:, 0:SEQ], rden[:], ALU.mult).then_inc(s["y_ready"], 1)

                    dve.wait_ge(x_loaded, 16)
                    layer_norm(1, x_in, x_hat, hat_ready)
                    dve.wait_ge(hat_t, 1)
                    nc.vector.tensor_scalar(x_t[0][:], front[:, 0, :], gamma[:, 0:1], beta[:, 0:1], ALU.mult, ALU.add).then_inc(xt_ready, 1)
                    attention(0)
                    dve.wait_ge(y_tr, 1)
                    nc.vector.tensor_tensor(x1[:].rearrange("p t e -> p (t e)"), x_in[:].rearrange("p t e -> p (t e)"),
                                            front[:, 0, :], ALU.add).then_inc(tok_read, 1)
                    dve.wait_ge(tok_read, 1)
                    layer_norm(2, x1, y1, hat_ready)
                    rms_norm(3, 1, y1, x_hat)
                    dve.wait_ge(head_sq, 1)
                    link(nc.vector.tensor_reduce(head_rr[:], sq[:].rearrange("p (a c) -> p a c", c=D), AX_X, ALU.add))
                    nc.vector.tensor_scalar(head_ss[:], head_rr[:], 1.0 / D, RMS_EPS, ALU.mult, ALU.add).then_inc(head_sum, 1)
                    dve.wait_ge(head_root, 1)
                    link(nc.vector.reciprocal(head_rr[:], head_rt[:]))
                    link(nc.vector.tensor_tensor(head_rg[:], head_rr[:], gain[:], ALU.mult))
                    for b in range(2):
                        nc.vector.tensor_tensor(qn[:, b * 256:(b + 1) * 256].rearrange("p (a c) -> p a c", c=D),
                                                front[:, b, 0:256].rearrange("p (a c) -> p a c", c=D),
                                                head_rg[:, b * 32:(b + 1) * 32].rearrange("p (a o) -> p a o", o=1).to_broadcast([P, 32, D]), ALU.mult)
                        ins = nc.vector.tensor_tensor(kn[:, b * 64:(b + 1) * 64].rearrange("p (a c) -> p a c", c=D),
                                                      front[:, b, 256:320].rearrange("p (a c) -> p a c", c=D),
                                                      head_rg[:, 64 + b * 8:64 + (b + 1) * 8].rearrange("p (a o) -> p a o", o=1).to_broadcast([P, 8, D]), ALU.mult)
                    link(ins)
                    for xn, xc, xs, cos, sin in ((kn, kc, ks, cos_k, sin_k), (qn, qc, qs, cos_q, sin_q)):
                        nc.vector.tensor_tensor(xc[:], xn[:], cos[:], ALU.mult)
                        halves = [t[:].rearrange("p (a h c) -> p a h c", h=2, c=4) for t in (xs, xn, sin)]
                        for h in range(2):
                            ins = nc.vector.tensor_tensor(halves[0][:, :, h, :], halves[1][:, :, 1 - h, :], halves[2][:, :, h, :], ALU.mult)
                        ins.then_inc(rope_mul, 1)
                    dve.wait_ge(rope_mul, 1)
                    for g in range(GROUPS):
                        ins = nc.vector.tensor_tensor(k_rot[:].rearrange("p (a c g) -> p a c g", c=D, g=4)[:, :, :, g],
                                                      kc[:].rearrange("p (a c) -> p a c", c=D),
                                                      ks[:].rearrange("p (a c) -> p a c", c=D), ALU.add)
                    ins.then_inc(rope_done, 1)
                    attention(1)
                    dve.wait_ge(wo_done, 1)
                    flat = [t[:].rearrange("p t e -> p (t e)") for t in (x2, y1, x3, x_out, x1)]
                    nc.vector.tensor_tensor(flat[0], flat[1], front[:, 0, :], ALU.add).then_inc(tok_read, 1)
                    rms_norm(4, 2, x2, x_hat)
                    for h in range(4):
                        dve.wait_ge(relu_done, h + 1)
                        nc.vector.tensor_tensor(hid_t[:, h, :], relu[:, h % 2, :], relu[:, h % 2, :], ALU.mult).then_inc(hid_ready, 1)
                    dve.wait_ge(pj_done, 1)
                    link(nc.vector.tensor_tensor(flat[2], flat[0], front[:, 0, :], ALU.add))
                    link(nc.vector.tensor_tensor(flat[4], flat[2], flat[1], ALU.add))
                    layer_norm(5, x1, x_out, out_ready)

                @block.tensor
                def _(pe):
                    ident = const("ident")

                    def strips_of(ap, b):
                        return ap.rearrange("p (s b n) -> p b s n", b=PAIR, n=STRIP)[:, b, :, :]

                    def transposes(src, bank, done, by_strips):
                        for t in range(TILES):
                            dst = front[:, bank, t * P:(t + 1) * P]
                            if by_strips:
                                b, half = divmod(t, 2)
                                dst = strips_of(front[:, bank, :], b)[:, 4 * half:4 * half + 4, :]
                            mm = pe.transpose(dst, src[:, t, :], ident)
                        mm.then_inc(done, 1)

                    def values(l):
                        for st in range(PAIR * STRIPS):
                            b, strip = divmod(st, STRIPS)
                            toks = strips_of(x_t[l][:], b)[:, strip, :]
                            for j in range(QUADS):
                                mm = pe.matmul(pv_bank[32 * j:32 * j + 32, st * 32:st * 32 + 32], toks,
                                               wv_t[l][:, 32 * j:32 * j + 32], start=True, stop=True, skip_group_check=True)
                        mm.then_inc(L[l]["v_proj"], 1)

                    def attention(l):
                        s = L[l]

                        def scores(b, u):
                            n = b * NS + u
                            if n == 0:
                                pe.wait_ge(s["bd_ready"], 1)
                            if n >= S_RING:
                                pe.wait_ge(s["s_read"], n - S_RING + 1)
                            bank = score[:, n % S_RING, :]
                            first = True
                            for strip, g0, ng, off in S_UNITS[u]:
                                w = keys_of(strip)
                                for g in range(g0, g0 + ng):
                                    at = off + (g - g0) * w
                                    pe.matmul(bank[:, at:at + w], q_bd[:, g * 16 + strip * PAIR + b, :], strips_of(k_rows[0:ROWS, 0, g, :], b)[:, 0:strip + 1, :],
                                              start=first, stop=False, skip_group_check=True)
                                    first = False
                                dst = bank[:, off:off + ng * w].rearrange("p (g k) -> p g k", g=ng)[:, :, w - STRIP:w]
                                mm = pe.matmul(dst, ident_b[:], mask_s[:].rearrange("p (o k) -> p o k", o=1).to_broadcast([P, ng, STRIP]),
                                               start=False, stop=True, skip_group_check=True)
                            mm.then_inc(s["s_done"], 1)

                        def maxima(b):
                            pe.wait_ge(s["m_ready"], b + 1)
                            if b:
                                pe.wait_ge(s["m_copied"], b)
                            pe.transpose(front[0:64, 0, 0:64].bitcast(BF16), mx_parts[:, b].rearrange("p t n -> p (t n)"), ident_b[:]).then_inc(s["m_tr"], 1)

                        def scores_t(b, u):
                            n = b * NP + u
                            if n == 0:
                                pe.wait_ge(s["bd_ready"], 3)
                            if u == 0:
                                pe.wait_ge(s["m_in"], 64 * (b + 1))
                            if n >= T_RING:
                                pe.wait_ge(s["p_ready"], n - T_RING + 1)
                            bank = score_t[:, n % T_RING, :]
                            first = True
                            for strip, g0, ng, off in P_UNITS[u]:
                                w = queries_of(strip)
                                for g in range(g0, g0 + ng):
                                    at = off + (g - g0) * w
                                    for n_pass in range(2):
                                        pe.matmul(bank[:, at:at + w], k_bd[n_pass][:, g * 16 + strip * PAIR + b, :],
                                                  strips_of(q_rows[:, n_pass, g, :], b)[:, strip:, :],
                                                  start=first, stop=False, skip_group_check=True)
                                        first = False
                                dst = bank[:, off:off + ng * w].rearrange("p (g k) -> p g k", g=ng)[:, :, 0:STRIP]
                                mm = pe.matmul(dst, ident_b[:], mask_st[:].rearrange("p (o k) -> p o k", o=1).to_broadcast([P, ng, STRIP]),
                                               start=False, stop=True, skip_group_check=True)
                            mm.then_inc(s["t_done"], 1)

                        def product(b, pr):
                            units = [2 * pr, 2 * pr + 1] if pr < 4 else [8]
                            pe.wait_ge(s["p_ready"], b * NP + units[-1] + 1)
                            if b == 0 and pr == 0:
                                pe.wait_ge(s["v_ready"], 1)
                            bank = pv_bank if b == 0 else front[:, 1, :]
                            for r in range(len(P_UNITS[units[0]])):
                                for kind in range(2):
                                    for g in range(GROUPS):
                                        u = units[g // 2] if pr < 4 else 8
                                        strip, g0, ng, off = P_UNITS[u][r]
                                        w = queries_of(strip)
                                        at = off + (g - g0) * w
                                        lhs = v_bd[:, b * STRIPS + strip, g, :] if kind == 0 else const("ones_bd")
                                        mm = pe.matmul(bank[32 * g:32 * g + 32, kind * SEQ + STRIP * strip:(kind + 1) * SEQ], lhs,
                                                       probs[:, (b * NP + u) % P_RING, at:at + w],
                                                       start=(strip == 0 and kind == 0), stop=(pr == 4), skip_group_check=True)
                            mm.then_inc(s["pv_done"], 1)

                        for u in range(NS):
                            scores(0, u)
                        scores(1, 0)
                        scores(1, 1)
                        maxima(0)
                        su = 2
                        for u in range(NP):
                            if u == 0:
                                for _ in range(3):
                                    scores(1, su)
                                    su += 1
                            scores_t(0, u)
                            if su < NS:
                                scores(1, su)
                                su += 1
                            if u >= 2 and u % 2 == 0:
                                product(0, u // 2 - 1)
                        while su < NS:
                            scores(1, su)
                            su += 1
                        maxima(1)
                        product(0, 4)
                        for u in range(NP):
                            scores_t(1, u)
                            if u >= 2 and u % 2 == 0:
                                product(1, u // 2 - 1)
                        product(1, 4)

                    pe.wait_ge(hat_ready, 1)
                    transposes(x_hat, 0, hat_t, True)
                    pe.wait_ge(xt_ready, 1)
                    pe.matmul(front[:, 1, :], wk_t[:], x_t[0][:], start=True, stop=True).then_inc(L[0]["qk_proj"], 1)
                    pe.matmul(front[:, 0, :], wq_t[:], x_t[0][:], start=True, stop=True).then_inc(L[0]["qk_proj"], 1)
                    values(0)
                    attention(0)
                    pe.wait_ge(L[0]["y_ready"], 2)
                    for t in range(TILES):
                        mm = pe.transpose(front[:, 0, t * P:(t + 1) * P], y_t[:, t * P:(t + 1) * P], const("perm"))
                    mm.then_inc(y_tr, 1)
                    pe.wait_ge(hat_ready, 3)
                    transposes(x_hat, 0, hat_t, True)
                    pe.wait_ge(xt_ready, 2)
                    for t in range(TILES):
                        b, a = divmod(t, 2)
                        toks = x_t[1][:, t * P:(t + 1) * P]
                        pe.matmul(front[:, b, a * P:(a + 1) * P], toks, wqk_t[:, 0:P], start=True, stop=True, skip_group_check=True)
                        mm = pe.matmul(front[:, b, 256 + a * 32:256 + (a + 1) * 32], toks, wqk_t[:, P:], start=True, stop=True, skip_group_check=True)
                    mm.then_inc(proj_tok, 1)
                    values(1)
                    pe.wait_ge(rope_done, 2)
                    for src, bank in ((k_rot, 1), (q_rot, 0)):
                        for t in range(TILES):
                            mm = pe.transpose(front[:, bank, t * P:(t + 1) * P], src[:, t * P:(t + 1) * P], ident)
                        mm.then_inc(L[1]["qk_proj"], 1)
                    attention(1)
                    pe.wait_ge(L[1]["y_ready"], 2)
                    for t in range(TILES):
                        mm = pe.matmul(front[:, 0, t * P:(t + 1) * P], y_t[:, t * P:(t + 1) * P], wo_t[:], start=True, stop=True, skip_group_check=True)
                    mm.then_inc(wo_done, 1)
                    pe.wait_ge(hat_ready, 4)
                    transposes(x_hat, 1, hat_t, False)
                    pe.wait_ge(xt_ready, 3)
                    for h in range(4):
                        if h >= 2:
                            pe.wait_ge(relu_done, h - 1)
                        pe.matmul(score[:, h % 2, :], w_fc[:, h * P:(h + 1) * P], x_t[2][:], start=True, stop=True).then_inc(fc_done, 1)
                    pe.wait_ge(hid_ready, 4)
                    for t in range(TILES):
                        for h in range(4):
                            mm = pe.matmul(front[:, 0, t * P:(t + 1) * P], hid_t[:, h, t * P:(t + 1) * P], w_pj[:, h, :],
                                           start=(t == 0 and h == 0), stop=(h == 3), skip_group_check=True)
                    mm.then_inc(pj_done, 1)

            with nc.Block() as block:
                @block.gpsimd
                def _(pool):
                    for s in loop_sems:
                        pool.sem_clear(s)


_INS = {"x": "L0_attn_x", "gamma": "L0_attn_gamma", "beta": "L0_attn_beta", "w_qkv": "L0_attn_w_qkv",
        "wq": "L0_ffn_wq", "wk": "L0_ffn_wk", "wv": "L0_ffn_wv", "wo": "L0_ffn_wo",
        "q_gain": "L0_ffn_q_gain", "k_gain": "L0_ffn_k_gain",
        "fc_s1": "L0_ffn_fc_s1", "fc_s2": "L0_ffn_fc_s2", "fc_mix": "L0_ffn_fc_mix", "fc_logits": "L0_ffn_fc_logits",
        "pj_s1": "L0_ffn_pj_s1", "pj_s2": "L0_ffn_pj_s2", "pj_mix": "L0_ffn_pj_mix", "pj_logits": "L0_ffn_pj_logits"}


def _constants():
    import numpy as np

    c = np.zeros((P, CONST_COLS), np.float32)

    def part(name):
        return c[:, CONSTS[name][0]:CONSTS[name][1]]

    rows = np.arange(P)
    part("ident")[:] = np.eye(P, dtype=np.float32)
    g, j, d = rows // 32, rows % 32 // D, rows % D
    part("perm")[rows, 32 * j + D * g + d] = 1.0
    col = np.arange(STRIP)
    part("mask_s")[:] = np.where(col[None, :] > (rows % STRIP)[:, None], -3e38, 0.0)
    part("mask_st")[:] = np.where((rows % STRIP)[:, None] > col[None, :], -3e38, 0.0)
    part("quad")[:] = (rows // D % QUADS)[:, None] == np.arange(QUADS)[None, :]
    part("ones_bd")[:] = (rows // STRIP)[:, None] == (col // D)[None, :]
    part("negsel")[ROWS:MROWS] = -((rows // STRIP)[None, :] == np.arange(QUADS)[:, None]).astype(np.float32)
    t = np.arange(SEQ, dtype=np.float32)
    inv = (1.0 / np.float32(10000.0) ** (np.arange(0, D, 2, dtype=np.float32) / np.float32(D))).astype(np.float32)
    place = (2 * np.arange(TILES)[None, :] + (rows // (2 * STRIP))[:, None]) * STRIP + (rows % STRIP)[:, None]
    angle = np.outer(t, inv).astype(np.float32)[place]
    part("cos")[:] = np.concatenate([np.cos(angle), np.cos(angle)], -1).reshape(P, TILES * D)
    part("sin")[:] = np.concatenate([np.sin(angle), -np.sin(angle)], -1).reshape(P, TILES * D)
    part("ones")[:] = 1.0
    return c


def kernel(**inputs):
    import numpy as _np
    import concourse.bacc as _bacc
    from concourse import mybir as _mybir
    from concourse.bass_utils import run_bass_kernel_spmd as _run

    nc = _bacc.Bacc("TRN2", target_bir_lowering=False, num_devices=1)
    arrays, io = {}, {}
    for name, given in _INS.items():
        a = _np.ascontiguousarray(inputs[given])
        arrays[f"in_{name}"] = a
        io[name] = nc.dram_tensor(f"in_{name}", a.shape, _mybir.dt.from_np(a.dtype), kind="ExternalInput").ap()
    arrays["in_consts"] = _constants()
    io["consts"] = nc.dram_tensor("in_consts", (P, CONST_COLS), _mybir.dt.float32, kind="ExternalInput").ap()
    out = nc.dram_tensor("out_x", (BATCH, SEQ, E), _mybir.dt.float32, kind="ExternalOutput").ap()
    build(nc, io, out)
    r = _run(nc, [arrays], core_ids=[0])
    return r.results[0]["out_x"]
```

```python
from contextlib import ExitStack

import concourse.bass as bass
from concourse import mybir

F32 = mybir.dt.float32
BF16 = mybir.dt.bfloat16
U32 = mybir.dt.uint32
ALU = mybir.AluOpType
ACT = mybir.ActivationFunctionType
AX_X = mybir.AxisListType.X

P = 128
BATCH, SEQ, E = 8, 256, 128
HEADS, KV_HEADS, D = 16, 4, 8
GROUPS, QUADS = 4, 4
STRIP = 32
STRIPS = SEQ // STRIP
STREAMS = 4
TURNS = BATCH // STREAMS
TILES = SEQ // P
NHT = TILES * (HEADS + KV_HEADS)
ROWS = 3 * STRIP
MROWS = ROWS + QUADS
HID, BLK, BANK, TOPK = 512, 64, 8, 2
NB_IN = {"fc": E // BLK, "pj": HID // BLK}
SCALE = float(D) ** -0.5
LN_EPS, RMS_EPS = 1e-5, 1e-6

CONSTS = {}
_at = 0
for _name, _width in (("ident", P), ("perm", P), ("mask_s", STRIP), ("mask_st", STRIP), ("quad", QUADS),
                      ("ones_bd", STRIP), ("negsel", P), ("cos", TILES * D), ("sin", TILES * D), ("ones", BLK)):
    CONSTS[_name] = (_at, _at + _width)
    _at += _width
CONST_COLS = _at


def score_units():
    units = []
    for s in (7, 6, 5, 4):
        units += [[(s, 0, 2, 0)], [(s, 2, 2, 0)]]
    units += [[(3, 0, 4, 0)], [(2, 0, 4, 0)], [(1, 0, 4, 0), (0, 0, 4, 256)]]
    return units


def prob_units():
    units = []
    for a, b in ((0, None), (1, 7), (2, 6), (3, 5)):
        for g in (0, 2):
            unit = [(a, g, 2, 0)]
            if b is not None:
                unit.append((b, g, 2, 2 * (SEQ - STRIP * a)))
            units.append(unit)
    units.append([(4, 0, 4, 0)])
    return units


S_UNITS, P_UNITS = score_units(), prob_units()
NS, NP = len(S_UNITS), len(P_UNITS)
S_RING, T_RING, P_RING = 2, 3, 4

BLOCK_TICKS = 14
CORES = 2 * STREAMS
MAX_TICK = NS
T_START = 3
S_USES = NS + 1

_SPLIT = [(0, "act", "high"), (1, "dve", "resid"), (1, "sp", "rows_high"), (2, "act", "mid"), (3, "sp", "rows_mid"),
          (3, "dve", "low"), (4, "sp", "rows_low"), (7, "dve", "bd_q"), (8, "dve", "bd_k0"), (9, "dve", "bd_k1")]
CHAINS = {
    "front": [(0, "sp", "load"), (2, "dve", "ln_stats"), (2, "pool", "ln_root"), (3, "dve", "ln_out"), (3, "pe", "tr"),
              (4, "dve", "xt"), (4, "pe", "proj"), (5, "pe", "proj_v"), (6, "act", "vbd")]
             + [(5 + t, e, s) for t, e, s in _SPLIT],
    "middle": [(0, "pe", "perm"), (1, "dve", "residual"), (1, "dve", "ln_stats"), (1, "pool", "ln_root"), (2, "dve", "ln_out"),
               (2, "act", "squares"), (3, "dve", "rms_var"), (3, "pool", "rms_root"), (4, "dve", "rms_hat"), (4, "pe", "tr"),
               (5, "act", "xt"), (5, "pe", "proj_tok"), (6, "act", "tok_copy"), (6, "pe", "proj_v"), (7, "act", "vbd"),
               (7, "dve", "head_sums"), (7, "pool", "head_root"), (11, "dve", "head_norm"), (11, "pool", "rope_cos"),
               (12, "dve", "rope_sin"), (12, "pool", "rope_add"), (13, "pe", "tr_qk")]
              + [(14 + t, e, s) for t, e, s in _SPLIT],
    "end": [(0, "pe", "wo"), (1, "dve", "residual"), (1, "act", "squares"), (1, "pool", "sum2"), (2, "dve", "rms_var"),
            (2, "pool", "rms_root"), (3, "dve", "rms_hat"), (3, "pe", "tr"), (4, "act", "xt"), (4, "pe", "fc0"),
            (5, "act", "relu0"), (5, "pool", "square0"), (5, "pe", "fc1"), (6, "act", "relu1"), (6, "pool", "square1"),
            (7, "pe", "pj"), (8, "dve", "last_sum"), (8, "dve", "ln_stats"), (8, "pool", "ln_root"), (9, "dve", "ln_out"),
            (10, "sp", "store")],
}
FRONT_STEPS = ("perm", "tr", "proj", "proj_v", "proj_tok", "tr_qk", "wo", "fc0", "fc1", "pj")


class Schedule:

    def __init__(self, chains, cores):
        self.cores = cores
        self.keys = [(kind, q) for _, kind, q in chains]
        steps = [(start + t, n, i, engine, step, (kind, q)) for n, (start, kind, q) in enumerate(chains)
                 for i, (t, engine, step) in enumerate(CHAINS[kind])]
        self.steps = sorted(steps, key=lambda s: s[:3])
        self.ticks = self.steps[-1][0] + 1
        self.count, self.use, taken, used = {}, {}, {}, [0, 0]
        for _, _, _, _, step, key in self.steps:
            taken[step] = taken.get(step, 0) + 1
            self.count[step, key] = taken[step]
            if step in FRONT_STEPS:
                bank = sum(used) % 2
                used[bank] += 1
                self.use[step, key] = (bank, used[bank])

    def at(self, tick, engine):
        return [(step, key) for t, _, _, e, step, key in self.steps if t == tick and e == engine]


PROLOGUE = Schedule([(0, "front", 0), (3, "front", 1)], 0)
LOOP = Schedule([(0, "front", 2), (BLOCK_TICKS, "front", 3)]
                + [((q + 2) * BLOCK_TICKS, "middle", q) for q in range(STREAMS)]
                + [((q + 6) * BLOCK_TICKS, "end", q) for q in range(STREAMS)]
                + [(7 * BLOCK_TICKS + 6, "front", 0), (8 * BLOCK_TICKS + 6, "front", 1)], CORES)


def keys_of(s):
    return STRIP * (s + 1)


def queries_of(s):
    return SEQ - STRIP * s


def build(nc, io, out):
    with ExitStack() as ctx:
        def sb(name, shape, dt=F32):
            return ctx.enter_context(nc.sbuf_tensor(name, shape, dt))

        def psum(name, shape, dt=F32):
            return ctx.enter_context(nc.psum_tensor(name, shape, dt))

        def sem(name):
            return ctx.enter_context(nc.semaphore(name))

        front = psum("front", [P, 2, 512])
        score = psum("score", [P, S_RING, 512])
        score_t = psum("score_t", [P, T_RING, 512])
        pv_bank = psum("pv_bank", [P, 512])

        cst = sb("cst", [P, CONST_COLS])

        def const(name):
            return cst[:, CONSTS[name][0]:CONSTS[name][1]]

        setup_ctx = ExitStack()

        def ts(name, shape, dt=F32):
            return setup_ctx.enter_context(nc.sbuf_tensor(name, shape, dt))

        ident_b = sb("ident_b", [P, P], BF16)
        mask_s = sb("mask_s", [P, STRIP], BF16)
        mask_st = sb("mask_st", [P, STRIP], BF16)
        negsel = sb("negsel", [P, P], BF16)
        gamma = sb("gamma", [P, 1])
        beta = sb("beta", [P, 1])
        gain = sb("gain", [P, NHT])
        cos_t, sin_t = sb("cos_t", [P, NHT * D]), sb("sin_t", [P, NHT * D])
        wq_t, wk_t = sb("wq_t", [P, P]), sb("wk_t", [P, P])
        wv_t = [sb(f"wv_t{l}", [P, P]) for l in range(2)]
        wqk_t = sb("wqk_t", [P, P + KV_HEADS * D])
        wo_t = sb("wo_t", [P, P])

        w_fc = sb("w_fc", [P, HID])
        w_pj = sb("w_pj", [P, 4, P])

        minus_half = sb("minus_half", [P, NHT])
        k_bd = [[sb(f"k_bd{q}_{n}", [MROWS, GROUPS * STRIPS, P], BF16) for n in range(2)] for q in range(STREAMS)]
        v_bd = [sb(f"v_bd{q}", [P, STRIPS, GROUPS, STRIP]) for q in range(STREAMS)]

        gain_in = ts("gain_in", [P, HEADS + KV_HEADS])
        w_raw = ts("w_raw", [P, 5, P])
        wkv_raw = ts("wkv_raw", [2 * KV_HEADS * D, P])
        wo_perm = ts("wo_perm", [P, P])
        logits = ts("logits", [1, 2, BANK])
        top_v = ts("top_v", [1, 2, 8])
        top_i = ts("top_i", [1, 2, 8], U32)
        coef = ts("coef", [1, 2, TOPK])
        coef_tmp = ts("coef_tmp", [1, 3, 2])
        coef_b = ts("coef_b", [BLK, 2 * TOPK])
        fc_mix_sb = [ts(f"fc_mix_sb{k}", [P, 4, P]) for k in range(TOPK)]
        fc_s2_sb = [ts(f"fc_s2_sb{k}", [P, 4, BLK]) for k in range(TOPK)]
        fc_s1_sb = [ts(f"fc_s1_sb{k}", [P, BLK]) for k in range(TOPK)]
        pj_mix_sb = [ts(f"pj_mix_sb{k}", [P, HID]) for k in range(TOPK)]
        pj_s2_sb = [ts(f"pj_s2_sb{k}", [P, BLK]) for k in range(TOPK)]
        pj_s1_sb = [ts(f"pj_s1_sb{k}", [P, 4, BLK]) for k in range(TOPK)]
        fc_s1_t = [ts(f"fc_s1_t{k}", [BLK, P]) for k in range(TOPK)]
        pj_s1_t = [ts(f"pj_s1_t{k}", [BLK, HID]) for k in range(TOPK)]
        twice = [ts(f"twice{m}", [BLK, 2, 1024]) for m in range(4)]
        rolled = [ts(f"rolled{m}", [BLK, 1024]) for m in range(4)]

        cst_in, w_in, small_in, logit_in, bank_in = (sem(n) for n in ("cst_in", "w_in", "small_in", "logit_in", "bank_in"))
        top_done, exp_done, coef_done, coefp_done, coefb_done = (sem(n) for n in ("top_done", "exp_done", "coef_done", "coefp_done", "coefb_done"))
        wo_ready, w_tr, w_ready, b16_ready, neg_in = (sem(n) for n in ("wo_ready", "w_tr", "w_ready", "b16_ready", "neg_in"))
        s1_tr, s1_ready, mixed, mix_read, roll_in, folded, fold_read = (sem(n) for n in ("s1_tr", "s1_ready", "mixed", "mix_read", "roll_in", "folded", "fold_read"))
        pool_set, set_chain = sem("pool_set"), sem("set_chain")

        with nc.Block() as block:
            @block.sync
            def _(sp):
                sp.dma_start(logits[:, 0, :], io["fc_logits"].rearrange("(a b) -> a b", a=1)).then_inc(logit_in, 16)
                sp.dma_start(logits[:, 1, :], io["pj_logits"].rearrange("(a b) -> a b", a=1)).then_inc(logit_in, 16)
                sp.dma_start(cst[:], io["consts"]).then_inc(cst_in, 16)
                sp.dma_start(w_raw[:, 0:3, :], io["w_qkv"].rearrange("(s p) e -> p s e", p=P)).then_inc(w_in, 16)
                sp.dma_start(w_raw[:, 3, :], io["wq"]).then_inc(w_in, 16)
                sp.dma_start(w_raw[:, 4, :], io["wo"]).then_inc(w_in, 16)
                sp.dma_start(wkv_raw[0:32, :], io["wk"]).then_inc(w_in, 16)
                sp.dma_start(wkv_raw[32:64, :], io["wv"]).then_inc(w_in, 16)
                sp.dma_start(gamma[:], io["gamma"].rearrange("(a b) -> a b", b=1)).then_inc(small_in, 16)
                sp.dma_start(beta[:], io["beta"].rearrange("(a b) -> a b", b=1)).then_inc(small_in, 16)
                sp.dma_start(gain_in[:, 0:HEADS], io["q_gain"].partition_broadcast(P)).then_inc(small_in, 16)
                sp.dma_start(gain_in[:, HEADS:], io["k_gain"].partition_broadcast(P)).then_inc(small_in, 16)
                sp.wait_ge(top_done, 2)
                member = []
                for w, kind in enumerate(("fc", "pj")):
                    for k in range(TOPK):
                        idx = sp.value_load(top_i[0:1, w, k:k + 1], min_val=0, max_val=BANK - 1)
                        member.append(idx)
                        if kind == "fc":
                            mix, s2, s1 = fc_mix_sb[k][:], fc_s2_sb[k][:], fc_s1_sb[k][:]
                            mix_d = io["fc_mix"].rearrange("a b c -> (a b) c")[bass.ds(idx * HID, HID)].rearrange("(t p) c -> p t c", p=P)
                            s2_d = io["fc_s2"].rearrange("a b c -> (a b) c")[bass.ds(idx * HID, HID)].rearrange("(t p) c -> p t c", p=P)
                            s1_d = io["fc_s1"].rearrange("a b c -> (a b) c")[bass.ds(idx * E, E)]
                        else:
                            mix, s2, s1 = pj_mix_sb[k][:], pj_s2_sb[k][:], pj_s1_sb[k][:]
                            mix_d = io["pj_mix"].rearrange("a b c -> (a b) c")[bass.ds(idx * E, E)]
                            s2_d = io["pj_s2"].rearrange("a b c -> (a b) c")[bass.ds(idx * E, E)]
                            s1_d = io["pj_s1"].rearrange("a b c -> (a b) c")[bass.ds(idx * HID, HID)].rearrange("(t p) c -> p t c", p=P)
                        sp.dma_start(mix, mix_d).then_inc(bank_in, 16)
                        sp.dma_start(s2, s2_d).then_inc(bank_in, 16)
                        sp.dma_start(s1, s1_d).then_inc(bank_in, 16)
                sp.wait_ge(b16_ready, 1)
                for q in range(STREAMS):
                    for n in range(2):
                        src = negsel[ROWS:MROWS, :].rearrange("p (o n) -> p o n", o=1).to_broadcast([QUADS, GROUPS * STRIPS, P])
                        sp.dma_start(k_bd[q][n][ROWS:MROWS, :, :], src).then_inc(neg_in, 16)
                for m in range(4):
                    sp.wait_ge(mix_read, 4 * (m + 1))
                    n_in = NB_IN["fc"] if m < 2 else NB_IN["pj"]
                    shift = (member[m] % n_in) * (1024 // n_in)
                    flat = twice[m][:].rearrange("p a n -> p (a n)")
                    sp.dma_start(rolled[m][:], flat[:, bass.ds(shift, 1024)]).then_inc(roll_in, 16)
                sp.wait_ge(neg_in, 16 * 2 * STREAMS)

            @block.gpsimd
            def _(pool):
                nc.gpsimd.memset(minus_half[:], -0.5)
                for q in range(STREAMS):
                    ins = nc.gpsimd.memset(v_bd[q][:], 0.0)
                ins.then_inc(pool_set, 1)
                pool.wait_ge(pool_set, 1)

            @block.scalar
            def _(act):
                act.wait_ge(coef_done, 1)
                nc.scalar.activation(coef_tmp[:, 1, :], coef_tmp[:, 0, :], ACT.Exp).then_inc(exp_done, 1)
                act.wait_ge(coefb_done, 1)
                for m in range(4):
                    act.wait_ge(mixed, m + 1)
                    w, k = divmod(m, TOPK)
                    for half in range(2):
                        src = score[0:BLK, half, :]
                        for rep in range(2):
                            if w == 0:
                                dst = twice[m][:, rep, :].rearrange("p (g t h e) -> p g t h e", g=2, t=4, h=2)[:, :, :, half, :]
                                s4 = src.rearrange("p (g t e) -> p g t e", g=2, t=4)
                            else:
                                dst = twice[m][:, rep, :].rearrange("p (g h e) -> p g h e", g=8, h=2)[:, :, half, :]
                                s4 = src.rearrange("p (g e) -> p g e", g=8)
                            nc.scalar.activation(dst, s4, ACT.Copy, scale=coef_b[:, m:m + 1]).then_inc(mix_read, 1)

            @block.vector
            def _(dve):
                n_chain = [0]

                def link(ins):
                    n_chain[0] += 1
                    ins.then_inc(set_chain, 1)
                    dve.wait_ge(set_chain, n_chain[0])

                dve.wait_ge(logit_in, 32)
                for w in range(2):
                    nc.vector.max(top_v[:, w, :], logits[:, w, :]).then_inc(set_chain, 1)
                    n_chain[0] += 1
                dve.wait_ge(set_chain, n_chain[0])
                for w in range(2):
                    nc.vector.max_index(top_i[:, w, :], top_v[:, w, :], logits[:, w, :]).then_inc(top_done, 1)
                nc.vector.tensor_tensor(coef_tmp[:, 0, :], top_v[:, :, 1], top_v[:, :, 0], ALU.subtract).then_inc(coef_done, 1)
                dve.wait_ge(exp_done, 1)
                link(nc.vector.tensor_scalar(coef_tmp[:, 2, :], coef_tmp[:, 1, :], 1.0, None, ALU.add))
                link(nc.vector.reciprocal(coef[:, :, 0], coef_tmp[:, 2, :]))
                nc.vector.tensor_tensor(coef[:, :, 1], coef[:, :, 0], coef_tmp[:, 1, :], ALU.mult).then_inc(coef_done, 1)
                dve.wait_ge(cst_in, 16)
                nc.vector.tensor_copy(ident_b[:], const("ident"))
                nc.vector.tensor_copy(mask_s[:], const("mask_s"))
                nc.vector.tensor_copy(mask_st[:], const("mask_st"))
                nc.vector.tensor_copy(negsel[:], const("negsel")).then_inc(b16_ready, 1)
                dve.wait_ge(w_in, 80)
                nc.vector.tensor_copy(wo_perm[:].rearrange("p (g j c) -> p j g c", g=4, j=4),
                                      w_raw[:, 4, :].rearrange("p (j g c) -> p j g c", j=4, g=4)).then_inc(wo_ready, 1)
                dve.wait_ge(small_in, 64)
                for name, full in (("cos", cos_t), ("sin", sin_t)):
                    for t in range(TILES):
                        one = const(name)[:, t * D:(t + 1) * D].rearrange("p (o c) -> p o c", o=1)
                        nc.vector.tensor_copy(full[:, t * P:(t + 1) * P].rearrange("p (h c) -> p h c", c=D),
                                              one.to_broadcast([P, HEADS, D]))
                        nc.vector.tensor_copy(full[:, SEQ + t * 32:SEQ + (t + 1) * 32].rearrange("p (h c) -> p h c", c=D),
                                              one.to_broadcast([P, KV_HEADS, D]))
                for at, h, src in ((0, HEADS, gain_in[:, 0:HEADS]), (TILES * HEADS, KV_HEADS, gain_in[:, HEADS:])):
                    nc.vector.tensor_copy(gain[:, at:at + TILES * h].rearrange("p (t h) -> p t h", t=TILES),
                                          src.rearrange("p (o h) -> p o h", o=1).to_broadcast([P, TILES, h]))
                dve.wait_ge(w_tr, 1)
                tr = front[:, 0, :].rearrange("p (s n) -> p s n", s=4)
                for w, dst in ((0, wq_t), (1, wk_t)):
                    nc.vector.tensor_copy(dst[:].rearrange("p (j c g) -> p j g c", j=4, c=D),
                                          tr[:, w, :].rearrange("p (j g c) -> p j g c", j=4, g=4))
                nc.vector.tensor_copy(wv_t[0][:], tr[:, 2, :])
                nc.vector.tensor_copy(wqk_t[:, 0:P], tr[:, 3, :])
                nc.vector.tensor_copy(wqk_t[:, P:P + 32], front[:, 1, 0:32])
                for g in range(GROUPS):
                    nc.vector.tensor_copy(wv_t[1][:].rearrange("p (j g c) -> p j g c", j=4, g=4)[:, :, g, :],
                                          front[:, 1, 32:64].rearrange("p (j c) -> p j c", j=4))
                nc.vector.tensor_copy(wo_t[:], front[:, 1, 128:256]).then_inc(w_ready, 1)
                dve.wait_ge(s1_tr, 1)
                for k in range(TOPK):
                    nc.vector.tensor_copy(fc_s1_t[k][:], pv_bank[0:BLK, k * P:(k + 1) * P])
                    nc.vector.tensor_copy(pj_s1_t[k][:], score_t[0:BLK, k, :])
                nc.vector.drain().then_inc(s1_ready, 1)
                dve.wait_ge(coefp_done, 1)
                nc.vector.tensor_copy(coef_b[:], score_t[0:BLK, 2, 0:4]).then_inc(coefb_done, 1)
                dve.wait_ge(folded, 1)
                nc.vector.tensor_copy(w_fc[:], front[:, 0, :])
                nc.vector.tensor_copy(w_pj[:].rearrange("p t n -> p (t n)"), front[:, 1, :]).then_inc(fold_read, 1)
                dve.wait_ge(fold_read, 1)

            @block.tensor
            def _(pe):
                pe.wait_ge(cst_in, 16)
                ident = const("ident")
                pe.wait_ge(coef_done, 2)
                pe.matmul(score_t[0:BLK, 2, 0:4], const("ones")[0:1, :], coef[:].rearrange("p a b -> p (a b)"),
                          start=True, stop=True).then_inc(coefp_done, 1)
                pe.wait_ge(w_in, 80)
                for s in range(4):
                    pe.transpose(front[:, 0, s * P:(s + 1) * P], w_raw[:, s, :], ident)
                pe.transpose(front[:, 1, 0:64], wkv_raw[:], ident[0:64, 0:64])
                pe.wait_ge(wo_ready, 1)
                pe.transpose(front[:, 1, 128:256], wo_perm[:], ident).then_inc(w_tr, 1)
                pe.wait_ge(bank_in, 16 * 12)
                for k in range(TOPK):
                    pe.transpose(pv_bank[0:BLK, k * P:(k + 1) * P], fc_s1_sb[k][:], ident)
                    for t in range(4):
                        mm = pe.transpose(score_t[0:BLK, k, t * P:(t + 1) * P], pj_s1_sb[k][:, t, :], ident)
                mm.then_inc(s1_tr, 1)
                for m in range(4):
                    w, k = divmod(m, TOPK)
                    if m:
                        pe.wait_ge(mix_read, 4 * m)
                    for half in range(2):
                        rows = slice(BLK * half, BLK * half + BLK)
                        for g in range(NB_IN["fc"] if w == 0 else NB_IN["pj"]):
                            if w == 0:
                                for t in range(4):
                                    mm = pe.matmul(score[0:BLK, half, (g * 4 + t) * BLK:(g * 4 + t + 1) * BLK],
                                                   fc_mix_sb[k][rows, t, :].rearrange("p (d g) -> p g d", g=2)[:, g, :],
                                                   fc_s2_sb[k][rows, t, :], start=True, stop=True)
                            else:
                                mm = pe.matmul(score[0:BLK, half, g * BLK:(g + 1) * BLK],
                                               pj_mix_sb[k][rows, :].rearrange("p (d g) -> p g d", g=8)[:, g, :],
                                               pj_s2_sb[k][rows, :], start=True, stop=True)
                    mm.then_inc(mixed, 1)
                pe.wait_ge(s1_ready, 1)
                pe.wait_ge(w_ready, 1)
                pe.wait_ge(roll_in, 64)
                for k in range(TOPK):
                    for g in range(2):
                        pe.matmul(front[BLK * g:BLK * g + BLK, 0, :], fc_s1_t[k][:, BLK * g:BLK * g + BLK],
                                  rolled[k][:, g * 512:(g + 1) * 512], start=(k == 0), stop=(k == 1), skip_group_check=True)
                for k in range(TOPK):
                    for g in range(8):
                        t, h = divmod(g, 2)
                        mm = pe.matmul(front[BLK * h:BLK * h + BLK, 1, t * P:(t + 1) * P],
                                       pj_s1_t[k][:, BLK * g:BLK * g + BLK], rolled[2 + k][:, g * P:(g + 1) * P],
                                       start=(k == 0 and t == 0), stop=(k == 1), skip_group_check=True)
                mm.then_inc(folded, 1)

        setup_ctx.close()

        def per_stream(name, shape, dt=F32):
            return [sb(f"{name}{q}", shape, dt) for q in range(STREAMS)]

        x_in, x_hat, x1, y1, x2 = (per_stream(n, [P, TILES, E]) for n in ("x_in", "x_hat", "x1_", "y1_", "x2_"))
        x_t, y_t = per_stream("x_t", [P, SEQ]), per_stream("y_t", [P, SEQ])
        q_rows = per_stream("q_rows", [MROWS, 2, GROUPS, SEQ], BF16)
        k_rows = per_stream("k_rows", [ROWS, GROUPS, SEQ], BF16)
        q_bd = per_stream("q_bd", [ROWS, GROUPS * STRIPS, P], BF16)
        bn, mv = per_stream("bn", [P, TILES, 6]), per_stream("mv", [P, TILES, 2])
        var_ln, rstd_ln = per_stream("var_ln", [P, TILES]), per_stream("rstd_ln", [P, TILES])
        sumsq, var_rms, rstd_rms = (per_stream(n, [P, TILES]) for n in ("sumsq", "var_rms", "rstd_rms"))
        junk = sb("junk", [P, E])
        parts = sb("parts", [P, 3, 2 * SEQ], BF16)
        qk_res = sb("qk_res", [P, 2 * SEQ])
        k_rows_p1 = sb("k_rows_p1", [ROWS, GROUPS, SEQ], BF16)
        qk_tok, qk_sq, qk_n = (sb(n, [P, NHT * D]) for n in ("qk_tok", "qk_sq", "qk_n"))
        qk_c, qk_s = qk_tok, qk_sq
        head_ss, head_var, head_rr, head_rg = (sb(n, [P, NHT]) for n in ("head_ss", "head_var", "head_rr", "head_rg"))
        rot = sb("rot", [P, 2 * SEQ])
        relu = sb("relu", [P, 2 * SEQ])
        hid_t = sb("hid_t", [P, 4, SEQ])
        mx = sb("mx", [P, GROUPS, STRIPS])
        mx_parts = sb("mx_parts", [P, 2, GROUPS * STRIPS], BF16)
        mx_t = sb("mx_t", [2 * GROUPS * STRIPS, P], BF16)
        probs = sb("probs", [P, P_RING, 512])
        rden = sb("rden", [P, SEQ])

        turn_sems = []

        def tsem(name):
            s = sem(name)
            turn_sems.append(s)
            return s

        done = {n: tsem(n + "_done") for n in (
            "ln_stats", "ln_root", "ln_out", "squares", "rms_var", "rms_root", "rms_hat", "high", "mid", "low",
            "vbd", "bd_q", "bd_k0", "bd_k1", "head_sums", "head_root", "head_norm", "rope_cos", "rope_sin", "rope_add",
            "sum2", "square0", "square1")}
        loaded = [tsem(f"loaded{q}") for q in range(STREAMS)]
        front_full = [tsem("front0_full"), tsem("front1_full")]
        front_read = [tsem("front0_read"), tsem("front1_read")]
        rows_q0, rows_k0, rows_p1, stored = (tsem(n) for n in ("rows_q0", "rows_k0", "rows_p1", "stored"))
        s_done, s_read, m_ready, m_in = (tsem(n) for n in ("s_done", "s_read", "m_ready", "m_in"))
        t_done, p_ready, pv_done, y_ready = (tsem(n) for n in ("t_done", "p_ready", "pv_done", "y_ready"))
        dve_order = tsem("dve_order")

        def flat(tile):
            return tile[:].rearrange("p t e -> p (t e)")

        def source(key):
            return "proj" if key[0] == "front" else "tr_qk"

        def sync_program(sp, plan, x_rows, o_rows):
            for tick in range(plan.ticks):
                for step, key in plan.at(tick, "sp"):
                    kind, q = key
                    n = plan.count[step, key]
                    if step == "load":
                        if plan.cores and q < 2:
                            sp.wait_ge(y_ready, STREAMS + q + 1)
                        sp.dma_start(x_in[q][:], x_rows[q]).then_inc(loaded[q], 16)
                    elif step == "store":
                        sp.wait_ge(done["ln_out"], plan.count["ln_out", key])
                        sp.dma_start(o_rows[q], x2[q][:]).then_inc(stored, 16)
                    else:
                        part, name, moves = {
                            "rows_high": (0, "high", ((q_rows, 0, 0), (q_rows, 0, 1), (k_rows, 0, 0), (k_rows, 0, 2), (k_rows, 1, 0), (q_rows, 1, 2))),
                            "rows_mid": (1, "mid", ((q_rows, 0, 2), (k_rows, 0, 1), (k_rows, 1, 1), (q_rows, 1, 1))),
                            "rows_low": (2, "low", ((k_rows, 1, 2), (q_rows, 1, 0)))}[step]
                        sp.wait_ge(done[name], plan.count[name, key])
                        if step == "rows_high" and n > 1:
                            sp.wait_ge(done["bd_k1"], n - 1)
                        for rows, n_pass, block in moves:
                            signal = rows_p1 if n_pass else (rows_q0 if rows is q_rows else rows_k0)
                            at = SEQ if rows is q_rows else 0
                            if rows is q_rows:
                                dst = q_rows[q][:, n_pass]
                            else:
                                dst = k_rows_p1[:] if n_pass else k_rows[q][:]
                            sp.dma_start(dst[32 * block:32 * block + 32], parts[:, part, at:at + SEQ]).then_inc(signal, 16)
                core, k = divmod(tick, BLOCK_TICKS)
                if core < plan.cores and k == MAX_TICK + 1:
                    sp.wait_ge(s_read, (core + 1) * S_USES)
                    for j in range(QUADS):
                        sp.dma_start(q_rows[core % STREAMS][ROWS + j:ROWS + j + 1].rearrange("p a g (s n) -> p (a g s) n", n=STRIP),
                                     mx_t[:, STRIP * j:STRIP * j + STRIP]).then_inc(m_in, 16)
            if plan.cores:
                sp.wait_ge(stored, 16 * STREAMS)

        def pool_program(pool, plan):
            for tick in range(plan.ticks):
                for step, key in plan.at(tick, "pool"):
                    kind, q = key
                    if step == "ln_root":
                        pool.wait_ge(done["ln_stats"], plan.count["ln_stats", key])
                        nc.gpsimd.tensor_tensor(rstd_ln[q][:], var_ln[q][:], minus_half[:, 0:TILES], ALU.pow).then_inc(done[step], 1)
                    elif step == "rms_root":
                        pool.wait_ge(done["rms_var"], plan.count["rms_var", key])
                        nc.gpsimd.tensor_tensor(rstd_rms[q][:], var_rms[q][:], minus_half[:, 0:TILES], ALU.pow).then_inc(done[step], 1)
                    elif step == "head_root":
                        pool.wait_ge(done["head_sums"], plan.count["head_sums", key])
                        nc.gpsimd.tensor_tensor(head_rr[:], head_var[:], minus_half[:], ALU.pow).then_inc(done[step], 1)
                    elif step == "rope_cos":
                        pool.wait_ge(done["head_norm"], plan.count["head_norm", key])
                        nc.gpsimd.tensor_tensor(qk_c[:], qk_n[:], cos_t[:], ALU.mult).then_inc(done[step], 1)
                    elif step == "rope_add":
                        pool.wait_ge(done["rope_cos"], plan.count["rope_cos", key])
                        pool.wait_ge(done["rope_sin"], plan.count["rope_sin", key])
                        nc.gpsimd.tensor_tensor(rot[:, SEQ:].rearrange("p (a c g) -> p a g c", c=D, g=4),
                                                qk_c[:, 0:SEQ].rearrange("p (a g c) -> p a g c", g=4, c=D),
                                                qk_s[:, 0:SEQ].rearrange("p (a g c) -> p a g c", g=4, c=D), ALU.add)
                        keys = [t[:, SEQ:].rearrange("p (a o c) -> p a o c", o=1, c=D).to_broadcast([P, 2 * QUADS, GROUPS, D]) for t in (qk_c, qk_s)]
                        nc.gpsimd.tensor_tensor(rot[:, 0:SEQ].rearrange("p (a c g) -> p a g c", c=D, g=4), keys[0], keys[1], ALU.add).then_inc(done[step], 1)
                    elif step == "sum2":
                        bank, n = plan.use["wo", key]
                        pool.wait_ge(front_read[bank], n)
                        nc.gpsimd.tensor_tensor(flat(x1[q]), flat(x2[q]), flat(y1[q]), ALU.add).then_inc(done[step], 1)
                    else:
                        half = int(step[-1])
                        bank, n = plan.use[f"fc{half}", key]
                        pool.wait_ge(front_read[bank], n)
                        nc.gpsimd.tensor_tensor(hid_t[:, 2 * half:2 * half + 2, :].rearrange("p h n -> p (h n)"), relu[:], relu[:], ALU.mult).then_inc(done[step], 1)

        def scalar_program(act, plan):
            for tick in range(plan.ticks):
                for step, key in plan.at(tick, "act"):
                    kind, q = key
                    n = plan.count[step, key]
                    if step == "squares":
                        if kind == "middle":
                            src = y1[q]
                            act.wait_ge(done["ln_out"], plan.count["ln_out", key])
                        else:
                            src = x2[q]
                            bank, use = plan.use["wo", key]
                            act.wait_ge(front_read[bank], use)
                        for t in range(TILES):
                            if TILES * (n - 1) + t:
                                act.wait_ge(done[step], TILES * (n - 1) + t)
                            nc.scalar.activation(junk[:], src[:, t, :], ACT.Square, accum_out=sumsq[q][:, t:t + 1]).then_inc(done[step], 1)
                    elif step == "xt":
                        bank, use = plan.use["tr", key]
                        act.wait_ge(front_full[bank], use)
                        nc.scalar.activation(x_t[q][:], front[:, bank, 0:SEQ], ACT.Copy).then_inc(front_read[bank], 1)
                    elif step == "tok_copy":
                        bank, use = plan.use["proj_tok", key]
                        act.wait_ge(front_full[bank], use)
                        if n > 1:
                            act.wait_ge(done["rope_add"], n - 1)
                        nc.scalar.activation(qk_sq[:], front[:, bank, 0:NHT * D], ACT.Square)
                        nc.scalar.activation(qk_tok[:], front[:, bank, 0:NHT * D], ACT.Copy).then_inc(front_read[bank], 1)
                    elif step == "vbd":
                        bank, use = plan.use["proj_v", key]
                        act.wait_ge(front_full[bank], use)
                        for j in range(QUADS):
                            r = slice(STRIP * j, STRIP * j + STRIP)
                            ins = nc.scalar.activation(v_bd[q][r, :, :, D * j:D * j + D],
                                                       front[r, bank, 0:SEQ].rearrange("p (s g c) -> p s g c", g=4, c=D), ACT.Copy)
                        ins.then_inc(front_read[bank], 1)
                    elif step == "high":
                        bank, use = plan.use[source(key), key]
                        act.wait_ge(front_full[bank], use)
                        if n > 1:
                            act.wait_ge(rows_q0, 48 * (n - 1))
                            act.wait_ge(rows_k0, 48 * (n - 1))
                            act.wait_ge(rows_p1, 96 * (n - 1))
                        nc.scalar.activation(parts[:, 0, :], front[:, bank, :], ACT.Copy).then_inc(done[step], 1)
                    elif step == "mid":
                        bank, use = plan.use[source(key), key]
                        act.wait_ge(front_read[bank], use)
                        nc.scalar.activation(parts[:, 1, :], qk_res[:], ACT.Copy).then_inc(done[step], 1)
                    else:
                        half = int(step[-1])
                        bank, use = plan.use[f"fc{half}", key]
                        act.wait_ge(front_full[bank], use)
                        if half:
                            act.wait_ge(done["square0"], n)
                        elif n > 1:
                            act.wait_ge(done["square1"], n - 1)
                        nc.scalar.activation(relu[:], front[:, bank, :], ACT.Relu).then_inc(front_read[bank], 1)
                core, u = tick // BLOCK_TICKS - 1, tick % BLOCK_TICKS - T_START
                if 0 <= core < plan.cores and 0 <= u < NP:
                    n = core * NP + u
                    act.wait_ge(t_done, n + 1)
                    if n >= P_RING:
                        c, v = divmod(n - P_RING, NP)
                        act.wait_ge(pv_done, c * 5 + v // 2 + 1)
                    nc.scalar.activation(probs[:, n % P_RING, :], score_t[:, n % T_RING, :], ACT.Exp, scale=SCALE).then_inc(p_ready, 1)

        def vector_program(dve, plan):
            n_order = [0]

            def link(ins):
                n_order[0] += 1
                ins.then_inc(dve_order, 1)
                dve.wait_ge(dve_order, n_order[0])

            def step_of(step, key):
                kind, q = key
                if step == "ln_stats":
                    if kind == "front":
                        dve.wait_ge(loaded[q], 16)
                        src = x_in[q]
                    else:
                        src = x1[q]
                    for t in range(TILES):
                        ins = nc.vector.bn_stats(bn[q][:, t, :], src[:, t, :])
                    link(ins)
                    for t in range(TILES):
                        ins = nc.vector.bn_aggr(mv[q][:, t, :], bn[q][:, t, :])
                    link(ins)
                    nc.vector.tensor_scalar(var_ln[q][:], mv[q][:, :, 1], LN_EPS, None, ALU.add).then_inc(done[step], 1)
                elif step == "ln_out":
                    src, dst = {"front": (x_in, x_hat), "middle": (x1, y1), "end": (x1, x2)}[kind]
                    dve.wait_ge(done["ln_root"], plan.count["ln_root", key])
                    for t in range(TILES):
                        ins = nc.vector.tensor_scalar(dst[q][:, t, :], src[q][:, t, :], mv[q][:, t, 0:1], rstd_ln[q][:, t:t + 1],
                                                      ALU.subtract, ALU.mult)
                    ins.then_inc(done[step], 1)
                elif step == "rms_var":
                    dve.wait_ge(done["squares"], TILES * plan.count["squares", key])
                    nc.vector.tensor_scalar(var_rms[q][:], sumsq[q][:], 1.0 / E, RMS_EPS, ALU.mult, ALU.add).then_inc(done[step], 1)
                elif step == "rms_hat":
                    dve.wait_ge(done["rms_root"], plan.count["rms_root", key])
                    src = y1[q] if kind == "middle" else x2[q]
                    for t in range(TILES):
                        ins = nc.vector.tensor_scalar(x_hat[q][:, t, :], src[:, t, :], rstd_rms[q][:, t:t + 1], None, ALU.mult)
                    ins.then_inc(done[step], 1)
                elif step == "xt":
                    bank, use = plan.use["tr", key]
                    dve.wait_ge(front_full[bank], use)
                    nc.vector.tensor_scalar(x_t[q][:], front[:, bank, 0:SEQ], gamma[:, 0:1], beta[:, 0:1], ALU.mult, ALU.add).then_inc(front_read[bank], 1)
                elif step == "residual":
                    bank, use = plan.use["perm" if kind == "middle" else "wo", key]
                    a, dst = (x_in, x1) if kind == "middle" else (y1, x2)
                    dve.wait_ge(front_full[bank], use)
                    nc.vector.tensor_tensor(flat(dst[q]), flat(a[q]), front[:, bank, 0:SEQ], ALU.add).then_inc(front_read[bank], 1)
                    dve.wait_ge(front_read[bank], use)
                elif step == "last_sum":
                    bank, use = plan.use["pj", key]
                    dve.wait_ge(front_full[bank], use)
                    dve.wait_ge(done["sum2"], plan.count["sum2", key])
                    nc.vector.tensor_tensor(flat(x1[q]), flat(x1[q]), front[:, bank, 0:SEQ], ALU.add).then_inc(front_read[bank], 1)
                    dve.wait_ge(front_read[bank], use)
                elif step == "head_sums":
                    bank, use = plan.use["proj_tok", key]
                    dve.wait_ge(front_read[bank], use)
                    link(nc.vector.tensor_reduce(head_ss[:], qk_sq[:].rearrange("p (a c) -> p a c", c=D), AX_X, ALU.add))
                    nc.vector.tensor_scalar(head_var[:], head_ss[:], 1.0 / D, RMS_EPS, ALU.mult, ALU.add).then_inc(done[step], 1)
                elif step == "head_norm":
                    dve.wait_ge(done["head_root"], plan.count["head_root", key])
                    link(nc.vector.tensor_tensor(head_rg[:], head_rr[:], gain[:], ALU.mult))
                    nc.vector.tensor_tensor(qk_n[:].rearrange("p (a c) -> p a c", c=D), qk_tok[:].rearrange("p (a c) -> p a c", c=D),
                                            head_rg[:].rearrange("p (a o) -> p a o", o=1).to_broadcast([P, NHT, D]), ALU.mult).then_inc(done[step], 1)
                    dve.wait_ge(done[step], plan.count[step, key])
                elif step == "rope_sin":
                    halves = [t[:].rearrange("p (a h c) -> p a h c", h=2, c=4) for t in (qk_s, qk_n, sin_t)]
                    for h in range(2):
                        ins = nc.vector.tensor_tensor(halves[0][:, :, h, :], halves[1][:, :, 1 - h, :], halves[2][:, :, h, :], ALU.mult)
                    ins.then_inc(done[step], 1)
                elif step == "resid":
                    bank, use = plan.use[source(key), key]
                    dve.wait_ge(done["high"], plan.count["high", key])
                    nc.vector.tensor_tensor(qk_res[:], front[:, bank, :], parts[:, 0, :], ALU.subtract).then_inc(front_read[bank], 1)
                elif step == "low":
                    dve.wait_ge(done["mid"], plan.count["mid", key])
                    nc.vector.tensor_tensor(parts[:, 2, :], qk_res[:], parts[:, 1, :], ALU.subtract).then_inc(done[step], 1)
                else:
                    signal, dmas, src, dst = {"bd_q": (rows_q0, 3, q_rows[q][0:ROWS, 0], q_bd[q]),
                                              "bd_k0": (rows_k0, 3, k_rows[q][:], k_bd[q][0]),
                                              "bd_k1": (rows_p1, 6, k_rows_p1[:], k_bd[q][1])}[step]
                    dve.wait_ge(signal, 16 * dmas * plan.count[step, key])
                    for j in range(QUADS):
                        ins = nc.vector.tensor_scalar(dst[0:ROWS, :, STRIP * j:STRIP * j + STRIP],
                                                      src.rearrange("p g (s n) -> p (g s) n", n=STRIP),
                                                      const("quad")[0:ROWS, j:j + 1], None, ALU.mult)
                    ins.then_inc(done[step], 1)

            for tick in range(plan.ticks):
                for step, key in plan.at(tick, "dve"):
                    step_of(step, key)
                core, k = divmod(tick, BLOCK_TICKS)
                if core < plan.cores and k < NS:
                    use = core * S_USES + k
                    dve.wait_ge(s_done, use + 1)
                    for strip, g0, ng, off in S_UNITS[k]:
                        w = keys_of(strip)
                        ins = nc.vector.tensor_reduce(mx[:, g0:g0 + ng, strip],
                                                      score[:, use % S_RING, off:off + ng * w].rearrange("p (g k) -> p g k", g=ng),
                                                      AX_X, ALU.max)
                    ins.then_inc(s_read, 1)
                if core < plan.cores and k == MAX_TICK:
                    dve.wait_ge(s_read, core * S_USES + NS)
                    all_mx = mx[:].rearrange("p g s -> p (g s)")
                    link(nc.vector.tensor_copy(mx_parts[:, 0, :], all_mx))
                    nc.vector.tensor_tensor(mx_parts[:, 1, :], all_mx, mx_parts[:, 0, :], ALU.subtract).then_inc(m_ready, 1)
                if core < plan.cores and k == MAX_TICK + 1:
                    use = core * S_USES + NS
                    dve.wait_ge(s_done, use + 1)
                    if core:
                        dve.wait_ge(m_in, 64 * core)
                    nc.vector.tensor_copy(mx_t[:], score[0:64, use % S_RING, 0:64].bitcast(BF16)).then_inc(s_read, 1)
                if 1 <= core <= plan.cores and k == MAX_TICK + 1:
                    dve.wait_ge(pv_done, core * 5)
                    link(nc.vector.reciprocal(rden[:], pv_bank[:, SEQ:]))
                    nc.vector.tensor_tensor(y_t[(core - 1) % STREAMS][:], pv_bank[:, 0:SEQ], rden[:], ALU.mult).then_inc(y_ready, 1)

        def tensor_program(pe, plan):
            ident = const("ident")

            def made_by(core):
                layer, q = divmod(core, STREAMS)
                return ("middle", q) if layer else (("front", q) if q >= 2 else None)

            def scores(core, u):
                q, use = core % STREAMS, core * S_USES + u
                if u == 0 and made_by(core):
                    pe.wait_ge(done["bd_k0"], plan.count["bd_k0", made_by(core)])
                if use >= S_RING:
                    pe.wait_ge(s_read, use - S_RING + 1)
                bank = score[:, use % S_RING, :]
                first = True
                for strip, g0, ng, off in S_UNITS[u]:
                    w = keys_of(strip)
                    for g in range(g0, g0 + ng):
                        at = off + (g - g0) * w
                        pe.matmul(bank[:, at:at + w], q_bd[q][:, g * STRIPS + strip, :], k_rows[q][:, g, 0:w],
                                  start=first, stop=False, skip_group_check=True)
                        first = False
                    dst = bank[:, off:off + ng * w].rearrange("p (g k) -> p g k", g=ng)[:, :, w - STRIP:w]
                    mm = pe.matmul(dst, ident_b[:], mask_s[:].rearrange("p (o k) -> p o k", o=1).to_broadcast([P, ng, STRIP]),
                                   start=False, stop=True, skip_group_check=True)
                mm.then_inc(s_done, 1)

            def scores_t(core, u):
                q, n = core % STREAMS, core * NP + u
                if u == 0:
                    pe.wait_ge(m_in, 64 * (core + 1))
                    if made_by(core):
                        pe.wait_ge(done["bd_k1"], plan.count["bd_k1", made_by(core)])
                if n >= T_RING:
                    pe.wait_ge(p_ready, n - T_RING + 1)
                bank = score_t[:, n % T_RING, :]
                first = True
                for strip, g0, ng, off in P_UNITS[u]:
                    w = queries_of(strip)
                    for g in range(g0, g0 + ng):
                        at = off + (g - g0) * w
                        for n_pass in range(2):
                            pe.matmul(bank[:, at:at + w], k_bd[q][n_pass][:, g * STRIPS + strip, :], q_rows[q][:, n_pass, g, STRIP * strip:],
                                      start=first, stop=False, skip_group_check=True)
                            first = False
                    dst = bank[:, off:off + ng * w].rearrange("p (g k) -> p g k", g=ng)[:, :, 0:STRIP]
                    mm = pe.matmul(dst, ident_b[:], mask_st[:].rearrange("p (o k) -> p o k", o=1).to_broadcast([P, ng, STRIP]),
                                   start=False, stop=True, skip_group_check=True)
                mm.then_inc(t_done, 1)

            def product(core, pr):
                q = core % STREAMS
                units = [2 * pr, 2 * pr + 1] if pr < 4 else [8]
                pe.wait_ge(p_ready, core * NP + units[-1] + 1)
                if pr == 0:
                    if core:
                        pe.wait_ge(y_ready, core)
                    if made_by(core):
                        bank, use = plan.use["proj_v", made_by(core)]
                        pe.wait_ge(front_read[bank], use)
                for r in range(len(P_UNITS[units[0]])):
                    for kind in range(2):
                        for g in range(GROUPS):
                            u = units[g // 2] if pr < 4 else 8
                            strip, g0, ng, off = P_UNITS[u][r]
                            w = queries_of(strip)
                            at = off + (g - g0) * w
                            lhs = v_bd[q][:, strip, g, :] if kind == 0 else const("ones_bd")
                            mm = pe.matmul(pv_bank[32 * g:32 * g + 32, kind * SEQ + STRIP * strip:(kind + 1) * SEQ], lhs,
                                           probs[:, (core * NP + u) % P_RING, at:at + w],
                                           start=(strip == 0 and kind == 0), stop=(pr == 4), skip_group_check=True)
                mm.then_inc(pv_done, 1)

            def step_of(step, key):
                kind, q = key
                bank, use = plan.use[step, key]
                dst = front[:, bank, :]
                if step == "perm":
                    pe.wait_ge(y_ready, q + 1)
                elif step == "wo":
                    pe.wait_ge(y_ready, STREAMS + q + 1)
                elif step == "tr":
                    stage = "ln_out" if kind == "front" else "rms_hat"
                    pe.wait_ge(done[stage], plan.count[stage, key])
                elif step in ("proj", "proj_v", "proj_tok", "fc0", "fc1"):
                    b, u = plan.use["tr", key]
                    pe.wait_ge(front_read[b], u)
                elif step == "tr_qk":
                    pe.wait_ge(done["rope_add"], plan.count["rope_add", key])
                elif step == "pj":
                    pe.wait_ge(done["square1"], plan.count["square1", key])
                if use > 1:
                    pe.wait_ge(front_read[bank], use - 1)
                layer = 0 if kind == "front" else 1
                if step in ("perm", "tr", "wo", "pj", "proj_tok"):
                    for t in range(TILES):
                        cols = slice(t * P, (t + 1) * P)
                        if step == "perm":
                            mm = pe.transpose(dst[:, cols], y_t[q][:, cols], const("perm"))
                        elif step == "tr":
                            mm = pe.transpose(dst[:, cols], x_hat[q][:, t, :], ident)
                        elif step == "wo":
                            mm = pe.matmul(dst[:, cols], y_t[q][:, cols], wo_t[:], start=(t == 0), stop=True, skip_group_check=True)
                        elif step == "proj_tok":
                            pe.matmul(dst[:, cols], x_t[q][:, cols], wqk_t[:, 0:P], start=(t == 0), stop=True, skip_group_check=True)
                            mm = pe.matmul(dst[:, SEQ + t * 32:SEQ + (t + 1) * 32], x_t[q][:, cols], wqk_t[:, P:], start=False, stop=True, skip_group_check=True)
                        else:
                            for h in range(4):
                                mm = pe.matmul(dst[:, cols], hid_t[:, h, cols], w_pj[:, h, :], start=(t == 0 and h == 0), stop=(h == 3), skip_group_check=True)
                elif step == "proj":
                    pe.matmul(dst[:, 0:SEQ], wk_t[:], x_t[q][:], start=True, stop=True, skip_group_check=True)
                    mm = pe.matmul(dst[:, SEQ:], wq_t[:], x_t[q][:], start=False, stop=True, skip_group_check=True)
                elif step == "tr_qk":
                    for t in range(2 * TILES):
                        mm = pe.transpose(dst[:, t * P:(t + 1) * P], rot[:, t * P:(t + 1) * P], ident)
                elif step == "proj_v":
                    for s in range(STRIPS):
                        for j in range(QUADS):
                            mm = pe.matmul(dst[32 * j:32 * j + 32, s * 32:s * 32 + 32], x_t[q][:, STRIP * s:STRIP * s + STRIP],
                                           wv_t[layer][:, 32 * j:32 * j + 32], start=True, stop=True, skip_group_check=True)
                else:
                    for i in range(2):
                        h = 2 * int(step[-1]) + i
                        mm = pe.matmul(dst[:, i * SEQ:(i + 1) * SEQ], w_fc[:, h * P:(h + 1) * P], x_t[q][:], start=(i == 0), stop=True, skip_group_check=True)
                mm.then_inc(front_full[bank], 1)

            for tick in range(plan.ticks):
                core, k = divmod(tick, BLOCK_TICKS)
                if core < plan.cores and k < NS:
                    scores(core, k)
                if core < plan.cores and k == MAX_TICK + 1:
                    pe.wait_ge(m_ready, core + 1)
                    use = core * S_USES + NS
                    pe.wait_ge(s_read, use - S_RING + 1)
                    pe.transpose(score[0:64, use % S_RING, 0:64].bitcast(BF16), mx_parts[:].rearrange("p t n -> p (t n)"), ident_b[:]).then_inc(s_done, 1)
                u = k - T_START
                if 1 <= core <= plan.cores:
                    if 0 <= u < NP:
                        scores_t(core - 1, u)
                    if u >= 2 and u % 2 == 0 and u < NP + 1:
                        product(core - 1, u // 2 - 1)
                    if u == NP:
                        product(core - 1, 4)
                for step, key in plan.at(tick, "pe"):
                    step_of(step, key)

        def clear_turn():
            with nc.Block() as block:
                @block.gpsimd
                def _(pool):
                    for s in turn_sems:
                        pool.sem_clear(s)

        x_flat = io["x"].rearrange("b n e -> (b n) e")
        o_flat = out.rearrange("b n e -> (b n) e")

        def rows_at(ap, at):
            return ap[bass.ds(at, SEQ)].rearrange("(t p) e -> p t e", p=P)

        with nc.Block() as block:
            @block.sync
            def _(sp):
                sync_program(sp, PROLOGUE, [rows_at(x_flat, 0), rows_at(x_flat, SEQ)], None)

            @block.gpsimd
            def _(pool):
                pool_program(pool, PROLOGUE)

            @block.scalar
            def _(act):
                scalar_program(act, PROLOGUE)

            @block.vector
            def _(dve):
                vector_program(dve, PROLOGUE)

            @block.tensor
            def _(pe):
                tensor_program(pe, PROLOGUE)
        clear_turn()

        with nc.Fori(0, TURNS) as turn:
            here = turn * (STREAMS * SEQ)
            after = (turn * (STREAMS * SEQ) + STREAMS * SEQ) % (BATCH * SEQ)
            x_rows = [rows_at(x_flat, (after if q < 2 else here) + q * SEQ) for q in range(STREAMS)]
            o_rows = [rows_at(o_flat, here + q * SEQ) for q in range(STREAMS)]
            with nc.Block() as block:
                @block.sync
                def _(sp):
                    sync_program(sp, LOOP, x_rows, o_rows)

                @block.gpsimd
                def _(pool):
                    pool_program(pool, LOOP)

                @block.scalar
                def _(act):
                    scalar_program(act, LOOP)

                @block.vector
                def _(dve):
                    vector_program(dve, LOOP)

                @block.tensor
                def _(pe):
                    tensor_program(pe, LOOP)
            clear_turn()


_INS = {"x": "L0_attn_x", "gamma": "L0_attn_gamma", "beta": "L0_attn_beta", "w_qkv": "L0_attn_w_qkv",
        "wq": "L0_ffn_wq", "wk": "L0_ffn_wk", "wv": "L0_ffn_wv", "wo": "L0_ffn_wo",
        "q_gain": "L0_ffn_q_gain", "k_gain": "L0_ffn_k_gain",
        "fc_s1": "L0_ffn_fc_s1", "fc_s2": "L0_ffn_fc_s2", "fc_mix": "L0_ffn_fc_mix", "fc_logits": "L0_ffn_fc_logits",
        "pj_s1": "L0_ffn_pj_s1", "pj_s2": "L0_ffn_pj_s2", "pj_mix": "L0_ffn_pj_mix", "pj_logits": "L0_ffn_pj_logits"}


def _constants():
    import numpy as np

    c = np.zeros((P, CONST_COLS), np.float32)

    def part(name):
        return c[:, CONSTS[name][0]:CONSTS[name][1]]

    rows = np.arange(P)
    part("ident")[:] = np.eye(P, dtype=np.float32)
    g, j, d = rows // 32, rows % 32 // D, rows % D
    part("perm")[rows, 32 * j + D * g + d] = 1.0
    col = np.arange(STRIP)
    part("mask_s")[:] = np.where(col[None, :] > (rows % STRIP)[:, None], -3e38, 0.0)
    part("mask_st")[:] = np.where((rows % STRIP)[:, None] > col[None, :], -3e38, 0.0)
    part("quad")[:] = (rows // D % QUADS)[:, None] == np.arange(QUADS)[None, :]
    part("ones_bd")[:] = (rows // STRIP)[:, None] == (col // D)[None, :]
    part("negsel")[ROWS:MROWS] = -((rows // STRIP)[None, :] == np.arange(QUADS)[:, None]).astype(np.float32)
    t = np.arange(SEQ, dtype=np.float32)
    inv = (1.0 / np.float32(10000.0) ** (np.arange(0, D, 2, dtype=np.float32) / np.float32(D))).astype(np.float32)
    place = np.arange(TILES)[None, :] * P + rows[:, None]
    angle = np.outer(t, inv).astype(np.float32)[place]
    part("cos")[:] = np.concatenate([np.cos(angle), np.cos(angle)], -1).reshape(P, TILES * D)
    part("sin")[:] = np.concatenate([np.sin(angle), -np.sin(angle)], -1).reshape(P, TILES * D)
    part("ones")[:] = 1.0
    return c


def kernel(**inputs):
    import numpy as _np
    import concourse.bacc as _bacc
    from concourse import mybir as _mybir
    from concourse.bass_utils import run_bass_kernel_spmd as _run

    nc = _bacc.Bacc("TRN2", target_bir_lowering=False, num_devices=1)
    arrays, io = {}, {}
    for name, given in _INS.items():
        a = _np.ascontiguousarray(inputs[given])
        arrays[f"in_{name}"] = a
        io[name] = nc.dram_tensor(f"in_{name}", a.shape, _mybir.dt.from_np(a.dtype), kind="ExternalInput").ap()
    arrays["in_consts"] = _constants()
    io["consts"] = nc.dram_tensor("in_consts", (P, CONST_COLS), _mybir.dt.float32, kind="ExternalInput").ap()
    out = nc.dram_tensor("out_x", (BATCH, SEQ, E), _mybir.dt.float32, kind="ExternalOutput").ap()
    build(nc, io, out)
    r = _run(nc, [arrays], core_ids=[0])
    return r.results[0]["out_x"]
```

```python
from contextlib import ExitStack

import concourse.bass as bass
from concourse import mybir

F32 = mybir.dt.float32
BF16 = mybir.dt.bfloat16
U32 = mybir.dt.uint32
ALU = mybir.AluOpType
ACT = mybir.ActivationFunctionType
AX_X = mybir.AxisListType.X

P = 128
BATCH, SEQ, E = 8, 256, 128
HEADS, KV_HEADS, D = 16, 4, 8
GROUPS, QUADS = 4, 4
STRIP = 32
STRIPS = SEQ // STRIP
STREAMS = 4
TURNS = BATCH // STREAMS
TILES = SEQ // P
NHT = TILES * (HEADS + KV_HEADS)
ROWS = 3 * STRIP
MROWS = ROWS + QUADS
HID, BLK, BANK, TOPK = 512, 64, 8, 2
NB_IN = {"fc": E // BLK, "pj": HID // BLK}
SCALE = float(D) ** -0.5
LN_EPS, RMS_EPS = 1e-5, 1e-6

CONSTS = {}
_at = 0
for _name, _width in (("ident", P), ("perm", P), ("mask_s", STRIP), ("mask_st", STRIP), ("quad", QUADS),
                      ("ones_bd", STRIP), ("negsel", P), ("cos", TILES * D), ("sin", TILES * D), ("ones", BLK)):
    CONSTS[_name] = (_at, _at + _width)
    _at += _width
CONST_COLS = _at


def score_units():
    units = []
    for s in (7, 6, 5, 4):
        units += [[(s, 0, 2, 0)], [(s, 2, 2, 0)]]
    units += [[(3, 0, 4, 0)], [(2, 0, 4, 0)], [(1, 0, 4, 0), (0, 0, 4, 256)]]
    return units


def prob_units():
    units = []
    for a, b in ((0, None), (1, 7), (2, 6), (3, 5)):
        for g in (0, 2):
            unit = [(a, g, 2, 0)]
            if b is not None:
                unit.append((b, g, 2, 2 * (SEQ - STRIP * a)))
            units.append(unit)
    units.append([(4, 0, 4, 0)])
    return units


S_UNITS, P_UNITS = score_units(), prob_units()
NS, NP = len(S_UNITS), len(P_UNITS)
S_RING, T_RING, P_RING = 3, 2, 4

BLOCK_TICKS = 14
CORES = 2 * STREAMS
T_START = 3
UNIT_AT = {0: 0, 1: 1, 2: 2, 4: 3, 5: 4, 7: 5, 8: 6, 10: 7, 11: 8}
PRODUCT_AT = {3: 0, 6: 1, 9: 2, 12: 3, 13: 4}
T_TICKS = 14
S_USES = NS + 1

_SPLIT = [(0, "act", "high"), (1, "dve", "resid"), (1, "sp", "rows_high"), (2, "act", "mid"), (3, "sp", "rows_mid"),
          (3, "dve", "low"), (4, "sp", "rows_low"), (6, "dve", "bd_q"), (7, "dve", "bd_k0"),
          (9, "act", "bd_k1_0"), (10, "act", "bd_k1_1"), (11, "act", "bd_k1_2"), (12, "act", "bd_k1_3")]
CHAINS = {
    "load": [(0, "sp", "load")],
    "front": [(0, "dve", "ln_stats"), (0, "pool", "ln_root"), (1, "dve", "ln_out"), (2, "pe", "tr"),
              (3, "dve", "xt"), (4, "pe", "proj"), (6, "pe", "proj_v"), (7, "act", "vbd")]
             + [(5 + t, e, s) for t, e, s in _SPLIT],
    "middle": [(0, "pe", "perm"), (1, "dve", "residual"), (1, "dve", "ln_stats"), (1, "pool", "ln_root"), (2, "dve", "ln_out"),
               (2, "act", "squares"), (3, "dve", "rms_var"), (3, "pool", "rms_root"), (4, "dve", "rms_hat"), (5, "pe", "tr"),
               (6, "act", "xt"), (6, "pe", "proj_tok"), (7, "act", "tok_copy"), (7, "pe", "proj_v"), (8, "act", "vbd"),
               (8, "dve", "head_sums"), (8, "act", "head_root"), (10, "dve", "head_norm"), (10, "pool", "rope_cos"),
               (11, "dve", "rope_sin"), (11, "pool", "rope_add"), (13, "pe", "tr_qk")]
              + [(14 + t, e, s) for t, e, s in _SPLIT],
    "end": [(0, "pe", "wo"), (1, "dve", "residual"), (1, "act", "squares"), (1, "pool", "sum2"), (2, "dve", "rms_var"),
            (2, "pool", "rms_root"), (3, "dve", "rms_hat"), (4, "pe", "tr"), (5, "act", "xt"), (5, "pe", "fc0"),
            (6, "act", "relu0"), (6, "pe", "fc1"), (7, "dve", "square0"), (7, "act", "relu1"), (8, "dve", "square1"),
            (9, "pe", "pj"), (10, "dve", "last_sum"), (10, "dve", "ln_stats"), (10, "pool", "ln_root"), (11, "dve", "ln_out"),
            (12, "sp", "store")],
    "fold": [(0, "pe", "s1_tr"), (1, "dve", "s1_copy")]
            + [(m + t, e, f"{s}{m}") for m in range(2 * TOPK) for t, e, s in ((1, "pe", "mix"), (2, "act", "copy_a"), (2, "dve", "copy_b"), (3, "sp", "roll"))]
            + [(7, "pe", "fold_fc"), (8, "sp", "negatives"), (9, "pe", "fold_pj"), (10, "dve", "fold_copy"), (10, "pe", "fold_end")],
}
BD_K1 = ("bd_k1_0", "bd_k1_1", "bd_k1_2", "bd_k1_3")
FRONT_STEPS = ("perm", "tr", "proj", "proj_v", "proj_tok", "tr_qk", "wo", "fc0", "fc1", "pj")


class Schedule:

    def __init__(self, chains, maxima, products):
        self.keys = [(kind, q) for _, kind, q in chains]
        self.maxima, self.products = maxima, products
        steps = [(start + t, n, i, engine, step, (kind, q)) for n, (start, kind, q) in enumerate(chains)
                 for i, (t, engine, step) in enumerate(CHAINS[kind])]
        self.steps = sorted(steps, key=lambda s: s[:3])
        self.ticks = max([self.steps[-1][0] + 1] + [start + NS + 2 for start, _ in maxima] + [start + T_TICKS for start, _ in products])
        self.count, self.use, taken, used = {}, {}, {}, [0, 0]
        for _, _, _, _, step, key in self.steps:
            taken[step] = taken.get(step, 0) + 1
            self.count[step, key] = taken[step]
            if step in FRONT_STEPS:
                bank = sum(used) % 2
                used[bank] += 1
                self.use[step, key] = (bank, used[bank])

    def maxima_at(self, tick):
        return [(i, core, tick - start) for i, (start, core) in enumerate(self.maxima) if 0 <= tick - start <= NS + 1]

    def products_at(self, tick):
        return [(i, core, UNIT_AT.get(tick - start), PRODUCT_AT.get(tick - start))
                for i, (start, core) in enumerate(self.products) if 0 <= tick - start < T_TICKS]

    def at(self, tick, engine):
        return [(step, key) for t, _, _, e, step, key in self.steps if t == tick and e == engine]


PROLOGUE = Schedule([(0, "front", 0), (9, "front", 1), (8, "fold", 0)], [(18, CORES)], [])
CARRIED = STREAMS - 1
LOOP = Schedule([(0, "end", CARRIED), (0, "front", 2), (BLOCK_TICKS - 1, "front", 3)]
                + [((q + 1) * BLOCK_TICKS + T_START + 1, "middle", q) for q in range(STREAMS)]
                + [((q + 5) * BLOCK_TICKS + T_START + 1, "end", q) for q in range(CARRIED)]
                + [((5 + min(q, 1)) * BLOCK_TICKS + 5, "load", q) for q in range(STREAMS)]
                + [(5 * BLOCK_TICKS + 12, "front", 0), (6 * BLOCK_TICKS + 12, "front", 1)],
                [(n * BLOCK_TICKS, n + 1) for n in range(CORES)],
                [(n * BLOCK_TICKS + (T_START if n else 0), n) for n in range(CORES)])
EPILOGUE = Schedule([(0, "end", CARRIED)], [], [])


def keys_of(s):
    return STRIP * (s + 1)


def queries_of(s):
    return SEQ - STRIP * s


def build(nc, io, out):
    with ExitStack() as ctx:
        def sb(name, shape, dt=F32):
            return ctx.enter_context(nc.sbuf_tensor(name, shape, dt))

        def psum(name, shape, dt=F32):
            return ctx.enter_context(nc.psum_tensor(name, shape, dt))

        def sem(name):
            return ctx.enter_context(nc.semaphore(name))

        front = psum("front", [P, 2, 512])
        score = psum("score", [P, S_RING, 512])
        score_t = psum("score_t", [P, T_RING, 512])
        pv_bank = psum("pv_bank", [P, 512])

        cst = sb("cst", [P, CONST_COLS])

        def const(name):
            return cst[:, CONSTS[name][0]:CONSTS[name][1]]

        setup_ctx = ExitStack()

        def ts(name, shape, dt=F32):
            return setup_ctx.enter_context(nc.sbuf_tensor(name, shape, dt))

        ident_b = sb("ident_b", [P, P], BF16)
        mask_s = sb("mask_s", [P, STRIP], BF16)
        mask_st = sb("mask_st", [P, STRIP], BF16)
        negsel = sb("negsel", [P, P], BF16)
        gamma = sb("gamma", [P, 1])
        beta = sb("beta", [P, 1])
        gain = sb("gain", [P, NHT])
        cos_t, sin_t = sb("cos_t", [P, NHT * D]), sb("sin_t", [P, NHT * D])
        wq_t, wk_t = sb("wq_t", [P, P]), sb("wk_t", [P, P])
        wv_t = [sb(f"wv_t{l}", [P, P]) for l in range(2)]
        wqk_t = sb("wqk_t", [P, P + KV_HEADS * D])
        wo_t = sb("wo_t", [P, P])

        w_fc = sb("w_fc", [P, HID])
        w_pj = sb("w_pj", [P, 4, P])

        minus_half = sb("minus_half", [P, NHT])
        k_bd = [[sb(f"k_bd{q}_{n}", [MROWS, GROUPS * STRIPS, P], BF16) for n in range(2)] for q in range(STREAMS)]
        v_bd = [sb(f"v_bd{q}", [P, STRIPS, GROUPS, STRIP]) for q in range(STREAMS)]

        def per_stream(name, shape, dt=F32):
            return [sb(f"{name}{q}", shape, dt) for q in first_streams]

        def streams():
            return {
                "x_hat": per_stream("x_hat", [P, TILES, E]),
                "x1": per_stream("x1_", [P, TILES, E]), "x2": per_stream("x2_", [P, TILES, E]),
                "x_t": per_stream("x_t", [P, SEQ]),
                "q_rows": per_stream("q_rows", [MROWS, 2, GROUPS, SEQ], BF16),
                "k_rows": per_stream("k_rows", [ROWS, GROUPS, SEQ], BF16),
                "q_bd": per_stream("q_bd", [ROWS, GROUPS * STRIPS, P], BF16),
                "sumsq": per_stream("sumsq", [P, TILES]), "var_rms": per_stream("var_rms", [P, TILES]),
                "rstd_rms": per_stream("rstd_rms", [P, TILES])}

        x_in = [sb(f"x_in{q}", [P, TILES, E]) for q in range(STREAMS)]
        y1 = [sb(f"y1_{q}", [P, TILES, E]) for q in range(STREAMS)]
        y_t = [sb(f"y_t{q}", [P, SEQ]) for q in range(STREAMS)]
        bn, mv, var_ln, rstd_ln = ([sb(f"{n}{q}", [P, TILES] + w) for q in range(2 * STREAMS)]
                                   for n, w in (("bn", [6]), ("mv", [2]), ("var_ln", []), ("rstd_ln", [])))
        first_streams = (0, 1)
        S = streams()
        parts = sb("parts", [P, 3, 2 * SEQ], BF16)
        qk_res = sb("qk_res", [P, 2 * SEQ])
        mx = sb("mx", [P, GROUPS, STRIPS])
        mx_parts = sb("mx_parts", [P, 2, GROUPS * STRIPS], BF16)
        mx_t = sb("mx_t", [2 * GROUPS * STRIPS, P], BF16)
        k_rows_p1 = sb("k_rows_p1", [ROWS, GROUPS, SEQ], BF16)

        gain_in = ts("gain_in", [P, HEADS + KV_HEADS])
        w_raw = ts("w_raw", [P, 5, P])
        wkv_raw = ts("wkv_raw", [2 * KV_HEADS * D, P])
        wo_perm = ts("wo_perm", [P, P])
        logits = ts("logits", [1, 2, BANK])
        top_v = ts("top_v", [1, 2, 8])
        top_i = ts("top_i", [1, 2, 8], U32)
        coef = ts("coef", [1, 2, TOPK])
        coef_tmp = ts("coef_tmp", [1, 3, 2])
        coef_b = ts("coef_b", [BLK, 2 * TOPK])
        fc_mix_sb = [ts(f"fc_mix_sb{k}", [P, 4, P]) for k in range(TOPK)]
        fc_s2_sb = [ts(f"fc_s2_sb{k}", [P, 4, BLK]) for k in range(TOPK)]
        fc_s1_sb = [ts(f"fc_s1_sb{k}", [P, BLK]) for k in range(TOPK)]
        pj_mix_sb = [ts(f"pj_mix_sb{k}", [P, HID]) for k in range(TOPK)]
        pj_s2_sb = [ts(f"pj_s2_sb{k}", [P, BLK]) for k in range(TOPK)]
        pj_s1_sb = [ts(f"pj_s1_sb{k}", [P, 4, BLK]) for k in range(TOPK)]
        fc_s1_t = [ts(f"fc_s1_t{k}", [BLK, P]) for k in range(TOPK)]
        pj_s1_t = [ts(f"pj_s1_t{k}", [BLK, HID]) for k in range(TOPK)]
        twice = [ts(f"twice{m}", [BLK, 2, 1024]) for m in range(2)]
        rolled = [ts(f"rolled{m}", [BLK, 1024]) for m in range(4)]

        setup_ctx.close()
        first_streams = (2, 3)
        for name, tiles in streams().items():
            S[name] += tiles
        x_hat, x1, x2, x_t = (S[n] for n in ("x_hat", "x1", "x2", "x_t"))
        q_rows, k_rows, q_bd = (S[n] for n in ("q_rows", "k_rows", "q_bd"))
        sumsq, var_rms, rstd_rms = (S[n] for n in ("sumsq", "var_rms", "rstd_rms"))
        junk = sb("junk", [P, E])
        qk_tok, qk_sq, qk_n = (sb(n, [P, NHT * D]) for n in ("qk_tok", "qk_sq", "qk_n"))
        qk_c, qk_s = qk_tok, qk_sq
        head_ss, head_var, head_rt, head_rr, head_rg = (sb(n, [P, NHT]) for n in ("head_ss", "head_var", "head_rt", "head_rr", "head_rg"))
        rot = sb("rot", [P, 2 * SEQ])
        relu = sb("relu", [P, 2 * SEQ])
        hid_t = sb("hid_t", [P, 4, SEQ])
        probs = sb("probs", [P, P_RING, 512])

        cst_in, wqkv_in, w_in, affine_in, gain_done, logit_in, bank_in = (sem(n) for n in (
            "cst_in", "wqkv_in", "w_in", "affine_in", "gain_in_done", "logit_in", "bank_in"))
        top_done, exp_done, coef_done, coefp_done, coefb_done = (sem(n) for n in ("top_done", "exp_done", "coef_done", "coefp_done", "coefb_done"))
        wqkv_tr, wo_ready, w_tr, w_ready, b16_ready, neg_in = (sem(n) for n in ("wqkv_tr", "wo_ready", "w_tr", "w_ready", "b16_ready", "neg_in"))
        s1_tr, s1_ready, mixed, read_a, read_b, folded, fold_read = (sem(n) for n in ("s1_tr", "s1_ready", "mixed", "read_a", "read_b", "folded", "fold_read"))
        roll_in = [sem(f"roll_in{m}") for m in range(2 * TOPK)]
        pool_set, set_chain = sem("pool_set"), sem("set_chain")

        turn_sems = []

        def tsem(name):
            s = sem(name)
            turn_sems.append(s)
            return s

        done = {n: tsem(n + "_done") for n in (
            "ln_stats", "ln_root", "ln_out", "squares", "rms_var", "rms_root", "rms_hat", "high", "mid", "low",
            "vbd", "bd_q", "bd_k0", "bd_k1_3", "head_sums", "head_root", "head_norm", "rope_cos", "rope_sin", "rope_add",
            "sum2", "square0", "square1")}
        loaded = [tsem(f"loaded{q}") for q in range(STREAMS)]
        front_full = [tsem("front0_full"), tsem("front1_full")]
        front_read = [tsem("front0_read"), tsem("front1_read")]
        rows_q0, rows_k0, rows_p1, stored = (tsem(n) for n in ("rows_q0", "rows_k0", "rows_p1", "stored"))
        s_done, s_read, m_ready, m_in = (tsem(n) for n in ("s_done", "s_read", "m_ready", "m_in"))
        t_done, p_ready, pv_done, y_ready = (tsem(n) for n in ("t_done", "p_ready", "pv_done", "y_ready"))
        dve_order = tsem("dve_order")

        def flat(tile):
            return tile[:].rearrange("p t e -> p (t e)")

        def stats_of(key):
            return key[1] + (STREAMS if key[0] == "front" else 0)

        def source(key):
            return "proj" if key[0] == "front" else "tr_qk"

        members = []

        def sync_setup(sp):
            sp.dma_start(logits[:, 0, :], io["fc_logits"].rearrange("(a b) -> a b", a=1)).then_inc(logit_in, 16)
            sp.dma_start(logits[:, 1, :], io["pj_logits"].rearrange("(a b) -> a b", a=1)).then_inc(logit_in, 16)
            sp.dma_start(cst[:], io["consts"]).then_inc(cst_in, 16)
            sp.dma_start(x_in[0][:], io["x"][0].rearrange("(t p) e -> p t e", p=P)).then_inc(loaded[0], 16)
            sp.dma_start(w_raw[:, 0:3, :], io["w_qkv"].rearrange("(s p) e -> p s e", p=P)).then_inc(wqkv_in, 16)
            sp.dma_start(gamma[:], io["gamma"].rearrange("(a b) -> a b", b=1)).then_inc(affine_in, 16)
            sp.dma_start(beta[:], io["beta"].rearrange("(a b) -> a b", b=1)).then_inc(affine_in, 16)
            sp.dma_start(w_raw[:, 3, :], io["wq"]).then_inc(w_in, 16)
            sp.dma_start(w_raw[:, 4, :], io["wo"]).then_inc(w_in, 16)
            sp.dma_start(wkv_raw[0:32, :], io["wk"]).then_inc(w_in, 16)
            sp.dma_start(wkv_raw[32:64, :], io["wv"]).then_inc(w_in, 16)
            sp.wait_ge(top_done, 2)
            for w, kind in enumerate(("fc", "pj")):
                for k in range(TOPK):
                    idx = sp.value_load(top_i[0:1, w, k:k + 1], min_val=0, max_val=BANK - 1)
                    members.append(idx)
                    if kind == "fc":
                        mix, s2, s1 = fc_mix_sb[k][:], fc_s2_sb[k][:], fc_s1_sb[k][:]
                        mix_d = io["fc_mix"].rearrange("a b c -> (a b) c")[bass.ds(idx * HID, HID)].rearrange("(t p) c -> p t c", p=P)
                        s2_d = io["fc_s2"].rearrange("a b c -> (a b) c")[bass.ds(idx * HID, HID)].rearrange("(t p) c -> p t c", p=P)
                        s1_d = io["fc_s1"].rearrange("a b c -> (a b) c")[bass.ds(idx * E, E)]
                    else:
                        mix, s2, s1 = pj_mix_sb[k][:], pj_s2_sb[k][:], pj_s1_sb[k][:]
                        mix_d = io["pj_mix"].rearrange("a b c -> (a b) c")[bass.ds(idx * E, E)]
                        s2_d = io["pj_s2"].rearrange("a b c -> (a b) c")[bass.ds(idx * E, E)]
                        s1_d = io["pj_s1"].rearrange("a b c -> (a b) c")[bass.ds(idx * HID, HID)].rearrange("(t p) c -> p t c", p=P)
                    sp.dma_start(mix, mix_d).then_inc(bank_in, 16)
                    sp.dma_start(s2, s2_d).then_inc(bank_in, 16)
                    sp.dma_start(s1, s1_d).then_inc(bank_in, 16)
            for q in range(1, STREAMS):
                sp.dma_start(x_in[q][:], io["x"][q].rearrange("(t p) e -> p t e", p=P)).then_inc(loaded[q], 16)
            sp.dma_start(gain_in[:, 0:HEADS], io["q_gain"].partition_broadcast(P)).then_inc(gain_done, 16)
            sp.dma_start(gain_in[:, HEADS:], io["k_gain"].partition_broadcast(P)).then_inc(gain_done, 16)

        def sync_negatives(sp):
            sp.wait_ge(b16_ready, 1)
            for q in range(STREAMS):
                for n in range(2):
                    src = negsel[ROWS:MROWS, :].rearrange("p (o n) -> p o n", o=1).to_broadcast([QUADS, GROUPS * STRIPS, P])
                    sp.dma_start(k_bd[q][n][ROWS:MROWS, :, :], src).then_inc(neg_in, 16)

        def pool_setup(pool):
            nc.gpsimd.memset(minus_half[:], -0.5).then_inc(pool_set, 1)
            for q in range(STREAMS):
                nc.gpsimd.memset(v_bd[q][:], 0.0).then_inc(pool_set, 1)
            nc.gpsimd.memset(y1[CARRIED][:], 0.0).then_inc(pool_set, 1)
            nc.gpsimd.memset(y_t[CARRIED][:], 0.0).then_inc(pool_set, 1)
            pool.wait_ge(pool_set, 3 + STREAMS)

        def scalar_setup(act):
            act.wait_ge(coef_done, 1)
            nc.scalar.activation(coef_tmp[:, 1, :], coef_tmp[:, 0, :], ACT.Exp).then_inc(exp_done, 1)
            act.wait_ge(pool_set, 1 + STREAMS)

        def vector_setup(dve):
            n_chain = [0]

            def link(ins):
                n_chain[0] += 1
                ins.then_inc(set_chain, 1)
                dve.wait_ge(set_chain, n_chain[0])

            dve.wait_ge(logit_in, 32)
            for w in range(2):
                nc.vector.max(top_v[:, w, :], logits[:, w, :]).then_inc(set_chain, 1)
                n_chain[0] += 1
            dve.wait_ge(set_chain, n_chain[0])
            for w in range(2):
                nc.vector.max_index(top_i[:, w, :], top_v[:, w, :], logits[:, w, :]).then_inc(top_done, 1)
            nc.vector.tensor_tensor(coef_tmp[:, 0, :], top_v[:, :, 1], top_v[:, :, 0], ALU.subtract).then_inc(coef_done, 1)
            dve.wait_ge(exp_done, 1)
            link(nc.vector.tensor_scalar(coef_tmp[:, 2, :], coef_tmp[:, 1, :], 1.0, None, ALU.add))
            link(nc.vector.reciprocal(coef[:, :, 0], coef_tmp[:, 2, :]))
            nc.vector.tensor_tensor(coef[:, :, 1], coef[:, :, 0], coef_tmp[:, 1, :], ALU.mult).then_inc(coef_done, 1)
            dve.wait_ge(cst_in, 16)
            nc.vector.tensor_copy(ident_b[:], const("ident"))
            nc.vector.tensor_copy(mask_s[:], const("mask_s"))
            nc.vector.tensor_copy(mask_st[:], const("mask_st"))
            nc.vector.tensor_copy(negsel[:], const("negsel")).then_inc(b16_ready, 1)
            dve.wait_ge(affine_in, 32)
            dve.wait_ge(wqkv_tr, 1)
            tr = front[:, 0, :].rearrange("p (s n) -> p s n", s=4)
            for w, dst in ((0, wq_t), (1, wk_t)):
                nc.vector.tensor_copy(dst[:].rearrange("p (j c g) -> p j g c", j=4, c=D),
                                      tr[:, w, :].rearrange("p (j g c) -> p j g c", j=4, g=4))
            nc.vector.tensor_copy(wv_t[0][:], tr[:, 2, :]).then_inc(w_ready, 1)
            dve.wait_ge(w_in, 64)
            nc.vector.tensor_copy(wo_perm[:].rearrange("p (g j c) -> p j g c", g=4, j=4),
                                  w_raw[:, 4, :].rearrange("p (j g c) -> p j g c", j=4, g=4)).then_inc(wo_ready, 1)

        def vector_fold(dve, step):
            if step == "s1_copy":
                dve.wait_ge(w_tr, 1)
                nc.vector.tensor_copy(wqk_t[:, 0:P], score[:, 0, 0:128])
                nc.vector.tensor_copy(wqk_t[:, P:P + 32], score[:, 0, 128:160])
                for g in range(GROUPS):
                    nc.vector.tensor_copy(wv_t[1][:].rearrange("p (j g c) -> p j g c", j=4, g=4)[:, :, g, :],
                                          score[:, 0, 160:192].rearrange("p (j c) -> p j c", j=4))
                nc.vector.tensor_copy(wo_t[:], score[:, 0, 256:384]).then_inc(w_ready, 1)
                dve.wait_ge(coefp_done, 1)
                nc.vector.tensor_copy(coef_b[:], score[0:BLK, 2, 0:4]).then_inc(coefb_done, 1)
                dve.wait_ge(s1_tr, 1)
                for k in range(TOPK):
                    nc.vector.tensor_copy(fc_s1_t[k][:], pv_bank[0:BLK, k * P:(k + 1) * P])
                    ins = nc.vector.tensor_copy(pj_s1_t[k][:], score_t[0:BLK, k, :])
                ins.then_inc(s1_ready, 1)
                dve.wait_ge(coefb_done, 1)
            elif step == "fold_copy":
                dve.wait_ge(folded, 2)
                nc.vector.tensor_copy(w_fc[:], score_t[:, 0, :])
                nc.vector.tensor_copy(w_pj[:].rearrange("p t n -> p (t n)"), pv_bank[:]).then_inc(fold_read, 1)
                for name, full in (("cos", cos_t), ("sin", sin_t)):
                    for t in range(TILES):
                        one = const(name)[:, t * D:(t + 1) * D].rearrange("p (o c) -> p o c", o=1)
                        nc.vector.tensor_copy(full[:, t * P:(t + 1) * P].rearrange("p (h c) -> p h c", c=D),
                                              one.to_broadcast([P, HEADS, D]))
                        nc.vector.tensor_copy(full[:, SEQ + t * 32:SEQ + (t + 1) * 32].rearrange("p (h c) -> p h c", c=D),
                                              one.to_broadcast([P, KV_HEADS, D]))
                dve.wait_ge(gain_done, 32)
                for at, h, src in ((0, HEADS, gain_in[:, 0:HEADS]), (TILES * HEADS, KV_HEADS, gain_in[:, HEADS:])):
                    ins = nc.vector.tensor_copy(gain[:, at:at + TILES * h].rearrange("p (t h) -> p t h", t=TILES),
                                                src.rearrange("p (o h) -> p o h", o=1).to_broadcast([P, TILES, h]))
                ins.then_inc(fold_read, 1)
                dve.wait_ge(fold_read, 2)
            else:
                m = int(step[-1])
                dve.wait_ge(mixed, m + 1)
                if m >= 2:
                    dve.wait_ge(roll_in[m - 2], 16)
                for rep in range(2):
                    ins = nc.vector.tensor_scalar(twice_at(m, 1, rep), mixed_at(m, 1), coef_b[:, m:m + 1], None, ALU.mult)
                ins.then_inc(read_b, 1)

        def scalar_fold(act, step):
            m = int(step[-1])
            act.wait_ge(coefb_done, 1)
            act.wait_ge(mixed, m + 1)
            if m >= 2:
                act.wait_ge(roll_in[m - 2], 16)
            for rep in range(2):
                ins = nc.scalar.activation(twice_at(m, 0, rep), mixed_at(m, 0), ACT.Copy, scale=coef_b[:, m:m + 1])
            ins.then_inc(read_a, 1)

        def sync_fold(sp, step):
            if step == "negatives":
                return sync_negatives(sp)
            m = int(step[-1])
            sp.wait_ge(read_a, m + 1)
            sp.wait_ge(read_b, m + 1)
            n_in = NB_IN["fc"] if m < 2 else NB_IN["pj"]
            shift = (members[m] % n_in) * (1024 // n_in)
            both = twice[m % 2][:].rearrange("p a n -> p (a n)")
            sp.dma_start(rolled[m][:], both[:, bass.ds(shift, 1024)]).then_inc(roll_in[m], 16)

        def mix_bank(m, half):
            return (score if m % 2 == 0 else score_t)[0:BLK, half, :]

        def mixed_at(m, half):
            if m < 2:
                return mix_bank(m, half).rearrange("p (g t e) -> p g t e", g=2, t=4)
            return mix_bank(m, half).rearrange("p (g e) -> p g e", g=8)

        def twice_at(m, half, rep):
            if m < 2:
                return twice[m % 2][:, rep, :].rearrange("p (g t h e) -> p g t h e", g=2, t=4, h=2)[:, :, :, half, :]
            return twice[m % 2][:, rep, :].rearrange("p (g h e) -> p g h e", g=8, h=2)[:, :, half, :]

        def tensor_setup(pe):
            pe.wait_ge(cst_in, 16)
            ident = const("ident")
            pe.wait_ge(wqkv_in, 16)
            for s in range(3):
                mm = pe.transpose(front[:, 0, s * P:(s + 1) * P], w_raw[:, s, :], ident)
            mm.then_inc(wqkv_tr, 1)
            pe.wait_ge(coef_done, 2)
            pe.matmul(score[0:BLK, 2, 0:4], const("ones")[0:1, :], coef[:].rearrange("p a b -> p (a b)"),
                      start=True, stop=True).then_inc(coefp_done, 1)
            pe.wait_ge(w_in, 64)
            pe.transpose(score[:, 0, 0:128], w_raw[:, 3, :], ident)
            pe.transpose(score[:, 0, 128:192], wkv_raw[:], ident[0:64, 0:64])
            pe.wait_ge(wo_ready, 1)
            pe.transpose(score[:, 0, 256:384], wo_perm[:], ident).then_inc(w_tr, 1)
            pe.wait_ge(w_ready, 1)

        def tensor_fold(pe, step):
            ident = const("ident")
            if step == "fold_end":
                pe.wait_ge(fold_read, 1)
            elif step == "s1_tr":
                pe.wait_ge(bank_in, 16 * 12)
                for k in range(TOPK):
                    pe.transpose(pv_bank[0:BLK, k * P:(k + 1) * P], fc_s1_sb[k][:], ident)
                    for t in range(4):
                        mm = pe.transpose(score_t[0:BLK, k, t * P:(t + 1) * P], pj_s1_sb[k][:, t, :], ident)
                mm.then_inc(s1_tr, 1)
            elif step == "fold_fc":
                pe.wait_ge(read_a, 2 * TOPK)
                pe.wait_ge(read_b, 2 * TOPK)
                for k in range(TOPK):
                    pe.wait_ge(roll_in[k], 16)
                    for g in range(2):
                        mm = pe.matmul(score_t[BLK * g:BLK * g + BLK, 0, :], fc_s1_t[k][:, BLK * g:BLK * g + BLK],
                                       rolled[k][:, g * 512:(g + 1) * 512], start=(k == 0), stop=(k == 1), skip_group_check=True)
                mm.then_inc(folded, 1)
            elif step == "fold_pj":
                for k in range(TOPK):
                    pe.wait_ge(roll_in[2 + k], 16)
                    for g in range(8):
                        t, h = divmod(g, 2)
                        mm = pe.matmul(pv_bank[BLK * h:BLK * h + BLK, t * P:(t + 1) * P],
                                       pj_s1_t[k][:, BLK * g:BLK * g + BLK], rolled[2 + k][:, g * P:(g + 1) * P],
                                       start=(k == 0 and t == 0), stop=(k == 1), skip_group_check=True)
                mm.then_inc(folded, 1)
            else:
                m = int(step[-1])
                w, k = divmod(m, TOPK)
                if m == 0:
                    pe.wait_ge(w_ready, 2)
                elif m == 1:
                    pe.wait_ge(s1_ready, 1)
                else:
                    pe.wait_ge(read_a, m - 1)
                    pe.wait_ge(read_b, m - 1)
                for half in range(2):
                    rows = slice(BLK * half, BLK * half + BLK)
                    for g in range(NB_IN["fc"] if w == 0 else NB_IN["pj"]):
                        if w == 0:
                            for t in range(4):
                                mm = pe.matmul(mix_bank(m, half)[:, (g * 4 + t) * BLK:(g * 4 + t + 1) * BLK],
                                               fc_mix_sb[k][rows, t, :].rearrange("p (d g) -> p g d", g=2)[:, g, :],
                                               fc_s2_sb[k][rows, t, :], start=True, stop=True)
                        else:
                            mm = pe.matmul(mix_bank(m, half)[:, g * BLK:(g + 1) * BLK],
                                           pj_mix_sb[k][rows, :].rearrange("p (d g) -> p g d", g=8)[:, g, :],
                                           pj_s2_sb[k][rows, :], start=True, stop=True)
                mm.then_inc(mixed, 1)

        def sync_program(sp, plan, x_rows, o_rows):
            for tick in range(plan.ticks):
                for step, key in plan.at(tick, "sp"):
                    kind, q = key
                    n = plan.count[step, key]
                    if kind == "fold":
                        sync_fold(sp, step)
                    elif step == "load":
                        if q < 2:
                            sp.wait_ge(y_ready, STREAMS + q + 1)
                        else:
                            bank, use = plan.use["perm", ("middle", q)]
                            sp.wait_ge(front_read[bank], use)
                        sp.dma_start(x_in[q][:], x_rows[q]).then_inc(loaded[q], 16)
                    elif step == "store":
                        sp.wait_ge(done["ln_out"], plan.count["ln_out", key])
                        sp.dma_start(o_rows[q], x2[q][:]).then_inc(stored, 16)
                    else:
                        name, moves = {
                            "rows_high": ("high", ((q_rows, 0, 0, 0), (q_rows, 0, 1, 0), (k_rows, 0, 0, 0), (k_rows, 0, 2, 0))),
                            "rows_mid": ("mid", ((q_rows, 0, 2, 1), (k_rows, 0, 1, 1))),
                            "rows_low": ("low", ((k_rows, 1, 0, 0), (k_rows, 1, 1, 1), (k_rows, 1, 2, 2),
                                                 (q_rows, 1, 0, 2), (q_rows, 1, 1, 1), (q_rows, 1, 2, 0)))}[step]
                        sp.wait_ge(done[name], plan.count[name, key])
                        if step == "rows_low" and n > 1:
                            sp.wait_ge(done["bd_k1_3"], n - 1)
                        for rows, n_pass, block, part in moves:
                            signal = rows_p1 if n_pass else (rows_q0 if rows is q_rows else rows_k0)
                            at = SEQ if rows is q_rows else 0
                            if rows is q_rows:
                                dst = q_rows[q][:, n_pass]
                            else:
                                dst = k_rows_p1[:] if n_pass else k_rows[q][:]
                            sp.dma_start(dst[32 * block:32 * block + 32], parts[:, part, at:at + SEQ]).then_inc(signal, 16)
                for i, core, u in plan.maxima_at(tick):
                    if u == NS + 1:
                        sp.wait_ge(s_read, (i + 1) * S_USES)
                        for j in range(QUADS):
                            sp.dma_start(q_rows[core % STREAMS][ROWS + j:ROWS + j + 1].rearrange("p a g (s n) -> p (a g s) n", n=STRIP),
                                         mx_t[:, STRIP * j:STRIP * j + STRIP]).then_inc(m_in, 16)
            if plan.maxima:
                sp.wait_ge(m_in, 64 * len(plan.maxima))
                for q in range(STREAMS):
                    sp.wait_ge(loaded[q], 16)
            if plan is not PROLOGUE:
                sp.wait_ge(stored, 16 * sum(kind == "end" for kind, _ in plan.keys))

        def pool_program(pool, plan):
            for tick in range(plan.ticks):
                for step, key in plan.at(tick, "pool"):
                    kind, q = key
                    if step == "ln_root":
                        st = stats_of(key)
                        pool.wait_ge(done["ln_stats"], plan.count["ln_stats", key])
                        nc.gpsimd.tensor_tensor(rstd_ln[st][:], var_ln[st][:], minus_half[:, 0:TILES], ALU.pow).then_inc(done[step], 1)
                    elif step == "rms_root":
                        pool.wait_ge(done["rms_var"], plan.count["rms_var", key])
                        nc.gpsimd.tensor_tensor(rstd_rms[q][:], var_rms[q][:], minus_half[:, 0:TILES], ALU.pow).then_inc(done[step], 1)
                    elif step == "rope_cos":
                        pool.wait_ge(done["head_norm"], plan.count["head_norm", key])
                        nc.gpsimd.tensor_tensor(qk_c[:], qk_n[:], cos_t[:], ALU.mult).then_inc(done[step], 1)
                    elif step == "rope_add":
                        pool.wait_ge(done["rope_cos"], plan.count["rope_cos", key])
                        pool.wait_ge(done["rope_sin"], plan.count["rope_sin", key])
                        nc.gpsimd.tensor_tensor(rot[:, SEQ:].rearrange("p (a c g) -> p a g c", c=D, g=4),
                                                qk_c[:, 0:SEQ].rearrange("p (a g c) -> p a g c", g=4, c=D),
                                                qk_s[:, 0:SEQ].rearrange("p (a g c) -> p a g c", g=4, c=D), ALU.add)
                        keys = [t[:, SEQ:].rearrange("p (a o c) -> p a o c", o=1, c=D).to_broadcast([P, 2 * QUADS, GROUPS, D]) for t in (qk_c, qk_s)]
                        nc.gpsimd.tensor_tensor(rot[:, 0:SEQ].rearrange("p (a c g) -> p a g c", c=D, g=4), keys[0], keys[1], ALU.add).then_inc(done[step], 1)
                    else:
                        bank, n = plan.use["wo", key]
                        pool.wait_ge(front_read[bank], n)
                        nc.gpsimd.tensor_tensor(flat(x1[q]), flat(x2[q]), flat(y1[q]), ALU.add).then_inc(done[step], 1)

        def scalar_program(act, plan):
            for tick in range(plan.ticks):
                for step, key in plan.at(tick, "act"):
                    if step in BD_K1:
                        continue
                    kind, q = key
                    n = plan.count[step, key]
                    if kind == "fold":
                        scalar_fold(act, step)
                    elif step == "squares":
                        if kind == "middle":
                            src = y1[q]
                            act.wait_ge(done["ln_out"], plan.count["ln_out", key])
                        else:
                            src = x2[q]
                            bank, use = plan.use["wo", key]
                            act.wait_ge(front_read[bank], use)
                        for t in range(TILES):
                            if TILES * (n - 1) + t:
                                act.wait_ge(done[step], TILES * (n - 1) + t)
                            nc.scalar.activation(junk[:], src[:, t, :], ACT.Square, accum_out=sumsq[q][:, t:t + 1]).then_inc(done[step], 1)
                    elif step == "xt":
                        bank, use = plan.use["tr", key]
                        act.wait_ge(front_full[bank], use)
                        nc.scalar.activation(x_t[q][:], front[:, bank, 0:SEQ], ACT.Copy).then_inc(front_read[bank], 1)
                    elif step == "tok_copy":
                        bank, use = plan.use["proj_tok", key]
                        act.wait_ge(front_full[bank], use)
                        if n > 1:
                            act.wait_ge(done["rope_add"], n - 1)
                        nc.scalar.activation(qk_sq[:], front[:, bank, 0:NHT * D], ACT.Square)
                        nc.scalar.activation(qk_tok[:], front[:, bank, 0:NHT * D], ACT.Copy).then_inc(front_read[bank], 1)
                    elif step == "vbd":
                        bank, use = plan.use["proj_v", key]
                        act.wait_ge(front_full[bank], use)
                        for j in range(QUADS):
                            r = slice(STRIP * j, STRIP * j + STRIP)
                            ins = nc.scalar.activation(v_bd[q][r, :, :, D * j:D * j + D],
                                                       front[r, bank, 0:SEQ].rearrange("p (s g c) -> p s g c", g=4, c=D), ACT.Copy)
                        ins.then_inc(front_read[bank], 1)
                    elif step == "high":
                        bank, use = plan.use[source(key), key]
                        act.wait_ge(front_full[bank], use)
                        if n > 1:
                            act.wait_ge(rows_q0, 48 * (n - 1))
                            act.wait_ge(rows_k0, 48 * (n - 1))
                            act.wait_ge(rows_p1, 96 * (n - 1))
                        nc.scalar.activation(parts[:, 0, :], front[:, bank, :], ACT.Copy).then_inc(done[step], 1)
                    elif step == "head_root":
                        act.wait_ge(done["head_sums"], plan.count["head_sums", key])
                        nc.scalar.activation(head_rt[:], head_var[:], ACT.Sqrt).then_inc(done[step], 1)
                    elif step == "mid":
                        bank, use = plan.use[source(key), key]
                        act.wait_ge(front_read[bank], use)
                        nc.scalar.activation(parts[:, 1, :], qk_res[:], ACT.Copy).then_inc(done[step], 1)
                    else:
                        half = int(step[-1])
                        bank, use = plan.use[f"fc{half}", key]
                        act.wait_ge(front_full[bank], use)
                        if half:
                            act.wait_ge(done["square0"], n)
                        elif n > 1:
                            act.wait_ge(done["square1"], n - 1)
                        nc.scalar.activation(relu[:], front[:, bank, :], ACT.Relu).then_inc(front_read[bank], 1)
                for i, core, u, _ in plan.products_at(tick):
                    if u is not None:
                        n = i * NP + u
                        act.wait_ge(t_done, n + 1)
                        if n >= P_RING:
                            c, v = divmod(n - P_RING, NP)
                            act.wait_ge(pv_done, c * 5 + v // 2 + 1)
                        nc.scalar.activation(probs[:, n % P_RING, :], score_t[:, n % T_RING, :], ACT.Exp, scale=SCALE).then_inc(p_ready, 1)
                for step, key in plan.at(tick, "act"):
                    if step in BD_K1:
                        j = BD_K1.index(step)
                        act.wait_ge(rows_p1, 96 * plan.count[step, key])
                        ins = nc.scalar.activation(k_bd[key[1]][1][0:ROWS, :, STRIP * j:STRIP * j + STRIP],
                                                   k_rows_p1[:].rearrange("p g (s n) -> p (g s) n", n=STRIP),
                                                   ACT.Copy, scale=const("quad")[0:ROWS, j:j + 1])
                        if j == QUADS - 1:
                            ins.then_inc(done[step], 1)

        def vector_program(dve, plan):
            n_order = [0]

            def link(ins):
                n_order[0] += 1
                ins.then_inc(dve_order, 1)
                dve.wait_ge(dve_order, n_order[0])

            def step_of(step, key):
                kind, q = key
                st = stats_of(key)
                if kind == "fold":
                    vector_fold(dve, step)
                elif step == "ln_stats":
                    if kind == "front":
                        if q < 2:
                            dve.wait_ge(loaded[q], 16)
                        src = x_in[q]
                    else:
                        src = x1[q]
                    for t in range(TILES):
                        ins = nc.vector.bn_stats(bn[st][:, t, :], src[:, t, :])
                    link(ins)
                    for t in range(TILES):
                        ins = nc.vector.bn_aggr(mv[st][:, t, :], bn[st][:, t, :])
                    link(ins)
                    nc.vector.tensor_scalar(var_ln[st][:], mv[st][:, :, 1], LN_EPS, None, ALU.add).then_inc(done[step], 1)
                elif step == "ln_out":
                    src, dst = {"front": (x_in, x_hat), "middle": (x1, y1), "end": (x1, x2)}[kind]
                    dve.wait_ge(done["ln_root"], plan.count["ln_root", key])
                    for t in range(TILES):
                        ins = nc.vector.tensor_scalar(dst[q][:, t, :], src[q][:, t, :], mv[st][:, t, 0:1], rstd_ln[st][:, t:t + 1],
                                                      ALU.subtract, ALU.mult)
                    ins.then_inc(done[step], 1)
                elif step == "rms_var":
                    dve.wait_ge(done["squares"], TILES * plan.count["squares", key])
                    nc.vector.tensor_scalar(var_rms[q][:], sumsq[q][:], 1.0 / E, RMS_EPS, ALU.mult, ALU.add).then_inc(done[step], 1)
                elif step == "rms_hat":
                    dve.wait_ge(done["rms_root"], plan.count["rms_root", key])
                    src = y1[q] if kind == "middle" else x2[q]
                    for t in range(TILES):
                        ins = nc.vector.tensor_scalar(x_hat[q][:, t, :], src[:, t, :], rstd_rms[q][:, t:t + 1], None, ALU.mult)
                    ins.then_inc(done[step], 1)
                elif step == "xt":
                    bank, use = plan.use["tr", key]
                    dve.wait_ge(front_full[bank], use)
                    nc.vector.tensor_scalar(x_t[q][:], front[:, bank, 0:SEQ], gamma[:, 0:1], beta[:, 0:1], ALU.mult, ALU.add).then_inc(front_read[bank], 1)
                elif step == "residual":
                    bank, use = plan.use["perm" if kind == "middle" else "wo", key]
                    a, dst = (x_in, x1) if kind == "middle" else (y1, x2)
                    dve.wait_ge(front_full[bank], use)
                    nc.vector.tensor_tensor(flat(dst[q]), flat(a[q]), front[:, bank, 0:SEQ], ALU.add).then_inc(front_read[bank], 1)
                    dve.wait_ge(front_read[bank], use)
                elif step == "last_sum":
                    bank, use = plan.use["pj", key]
                    dve.wait_ge(front_full[bank], use)
                    dve.wait_ge(done["sum2"], plan.count["sum2", key])
                    nc.vector.tensor_tensor(flat(x1[q]), flat(x1[q]), front[:, bank, 0:SEQ], ALU.add).then_inc(front_read[bank], 1)
                    dve.wait_ge(front_read[bank], use)
                elif step == "head_sums":
                    bank, use = plan.use["proj_tok", key]
                    dve.wait_ge(front_read[bank], use)
                    link(nc.vector.tensor_reduce(head_ss[:], qk_sq[:].rearrange("p (a c) -> p a c", c=D), AX_X, ALU.add))
                    nc.vector.tensor_scalar(head_var[:], head_ss[:], 1.0 / D, RMS_EPS, ALU.mult, ALU.add).then_inc(done[step], 1)
                elif step == "head_norm":
                    dve.wait_ge(done["head_root"], plan.count["head_root", key])
                    link(nc.vector.reciprocal(head_rr[:], head_rt[:]))
                    link(nc.vector.tensor_tensor(head_rg[:], head_rr[:], gain[:], ALU.mult))
                    nc.vector.tensor_tensor(qk_n[:].rearrange("p (a c) -> p a c", c=D), qk_tok[:].rearrange("p (a c) -> p a c", c=D),
                                            head_rg[:].rearrange("p (a o) -> p a o", o=1).to_broadcast([P, NHT, D]), ALU.mult).then_inc(done[step], 1)
                    dve.wait_ge(done[step], plan.count[step, key])
                elif step == "rope_sin":
                    halves = [t[:].rearrange("p (a h c) -> p a h c", h=2, c=4) for t in (qk_s, qk_n, sin_t)]
                    for h in range(2):
                        ins = nc.vector.tensor_tensor(halves[0][:, :, h, :], halves[1][:, :, 1 - h, :], halves[2][:, :, h, :], ALU.mult)
                    ins.then_inc(done[step], 1)
                elif step in ("square0", "square1"):
                    half = int(step[-1])
                    bank, use = plan.use[f"fc{half}", key]
                    dve.wait_ge(front_read[bank], use)
                    nc.vector.tensor_tensor(hid_t[:, 2 * half:2 * half + 2, :].rearrange("p h n -> p (h n)"), relu[:], relu[:], ALU.mult).then_inc(done[step], 1)
                elif step == "resid":
                    bank, use = plan.use[source(key), key]
                    dve.wait_ge(done["high"], plan.count["high", key])
                    nc.vector.tensor_tensor(qk_res[:], front[:, bank, :], parts[:, 0, :], ALU.subtract).then_inc(front_read[bank], 1)
                elif step == "low":
                    dve.wait_ge(done["mid"], plan.count["mid", key])
                    nc.vector.tensor_tensor(parts[:, 2, :], qk_res[:], parts[:, 1, :], ALU.subtract).then_inc(done[step], 1)
                else:
                    signal, src, dst = {"bd_q": (rows_q0, q_rows[q][0:ROWS, 0], q_bd[q]), "bd_k0": (rows_k0, k_rows[q][:], k_bd[q][0])}[step]
                    dve.wait_ge(signal, 48 * plan.count[step, key])
                    for j in range(QUADS):
                        ins = nc.vector.tensor_scalar(dst[0:ROWS, :, STRIP * j:STRIP * j + STRIP],
                                                      src.rearrange("p g (s n) -> p (g s) n", n=STRIP),
                                                      const("quad")[0:ROWS, j:j + 1], None, ALU.mult)
                    ins.then_inc(done[step], 1)

            for tick in range(plan.ticks):
                for step, key in plan.at(tick, "dve"):
                    if step not in ("bd_q", "bd_k0"):
                        step_of(step, key)
                for i, core, u in plan.maxima_at(tick):
                    use = i * S_USES + min(u, NS)
                    if u < NS:
                        dve.wait_ge(s_done, use + 1)
                        for strip, g0, ng, off in S_UNITS[u]:
                            w = keys_of(strip)
                            ins = nc.vector.tensor_reduce(mx[:, g0:g0 + ng, strip],
                                                          score[:, use % S_RING, off:off + ng * w].rearrange("p (g k) -> p g k", g=ng),
                                                          AX_X, ALU.max)
                        ins.then_inc(s_read, 1)
                    elif u == NS:
                        dve.wait_ge(s_read, use)
                        all_mx = mx[:].rearrange("p g s -> p (g s)")
                        link(nc.vector.tensor_copy(mx_parts[:, 0, :], all_mx))
                        nc.vector.tensor_tensor(mx_parts[:, 1, :], all_mx, mx_parts[:, 0, :], ALU.subtract).then_inc(m_ready, 1)
                    else:
                        dve.wait_ge(s_done, use + 1)
                        if i:
                            dve.wait_ge(m_in, 64 * i)
                        nc.vector.tensor_copy(mx_t[:], score[0:64, use % S_RING, 0:64].bitcast(BF16)).then_inc(s_read, 1)
                for i, core, _, pr in plan.products_at(tick):
                    if pr == 4:
                        dve.wait_ge(pv_done, (i + 1) * 5)
                        y = y_t[core % STREAMS]
                        link(nc.vector.reciprocal(y[:], pv_bank[:, SEQ:]))
                        nc.vector.tensor_tensor(y[:], pv_bank[:, 0:SEQ], y[:], ALU.mult).then_inc(y_ready, 1)
                for step, key in plan.at(tick, "dve"):
                    if step in ("bd_q", "bd_k0"):
                        step_of(step, key)

        def tensor_program(pe, plan):
            ident = const("ident")

            def made_by(core):
                if core < 2:
                    return None
                return ("middle" if STREAMS <= core < CORES else "front", core % STREAMS)

            def scores(i, core, u):
                q, use = core % STREAMS, i * S_USES + u
                if u == 0 and made_by(core):
                    pe.wait_ge(done["bd_k0"], plan.count["bd_k0", made_by(core)])
                if use >= S_RING:
                    pe.wait_ge(s_read, use - S_RING + 1)
                bank = score[:, use % S_RING, :]
                first = True
                for strip, g0, ng, off in S_UNITS[u]:
                    w = keys_of(strip)
                    for g in range(g0, g0 + ng):
                        at = off + (g - g0) * w
                        pe.matmul(bank[:, at:at + w], q_bd[q][:, g * STRIPS + strip, :], k_rows[q][:, g, 0:w],
                                  start=first, stop=False, skip_group_check=True)
                        first = False
                    dst = bank[:, off:off + ng * w].rearrange("p (g k) -> p g k", g=ng)[:, :, w - STRIP:w]
                    mm = pe.matmul(dst, ident_b[:], mask_s[:].rearrange("p (o k) -> p o k", o=1).to_broadcast([P, ng, STRIP]),
                                   start=False, stop=True, skip_group_check=True)
                mm.then_inc(s_done, 1)

            def scores_t(core, u):
                q, n = core % STREAMS, core * NP + u
                if u == 0:
                    if core:
                        pe.wait_ge(m_in, 64 * core)
                    if made_by(core):
                        pe.wait_ge(done["bd_k1_3"], plan.count["bd_k1_3", made_by(core)])
                if n >= T_RING:
                    pe.wait_ge(p_ready, n - T_RING + 1)
                bank = score_t[:, n % T_RING, :]
                first = True
                for strip, g0, ng, off in P_UNITS[u]:
                    w = queries_of(strip)
                    for g in range(g0, g0 + ng):
                        at = off + (g - g0) * w
                        for n_pass in range(2):
                            pe.matmul(bank[:, at:at + w], k_bd[q][n_pass][:, g * STRIPS + strip, :], q_rows[q][:, n_pass, g, STRIP * strip:],
                                      start=first, stop=False, skip_group_check=True)
                            first = False
                    dst = bank[:, off:off + ng * w].rearrange("p (g k) -> p g k", g=ng)[:, :, 0:STRIP]
                    mm = pe.matmul(dst, ident_b[:], mask_st[:].rearrange("p (o k) -> p o k", o=1).to_broadcast([P, ng, STRIP]),
                                   start=False, stop=True, skip_group_check=True)
                mm.then_inc(t_done, 1)

            def product(core, pr):
                q = core % STREAMS
                units = [2 * pr, 2 * pr + 1] if pr < 4 else [8]
                pe.wait_ge(p_ready, core * NP + units[-1] + 1)
                if pr == 0:
                    if core:
                        pe.wait_ge(y_ready, core)
                    if made_by(core):
                        bank, use = plan.use["proj_v", made_by(core)]
                        pe.wait_ge(front_read[bank], use)
                for r in range(len(P_UNITS[units[0]])):
                    for kind in range(2):
                        for g in range(GROUPS):
                            u = units[g // 2] if pr < 4 else 8
                            strip, g0, ng, off = P_UNITS[u][r]
                            w = queries_of(strip)
                            at = off + (g - g0) * w
                            lhs = v_bd[q][:, strip, g, :] if kind == 0 else const("ones_bd")
                            mm = pe.matmul(pv_bank[32 * g:32 * g + 32, kind * SEQ + STRIP * strip:(kind + 1) * SEQ], lhs,
                                           probs[:, (core * NP + u) % P_RING, at:at + w],
                                           start=(strip == 0 and kind == 0), stop=(pr == 4), skip_group_check=True)
                mm.then_inc(pv_done, 1)

            def step_of(step, key):
                kind, q = key
                bank, use = plan.use[step, key]
                dst = front[:, bank, :]
                if step == "perm":
                    pe.wait_ge(y_ready, q + 1)
                elif step == "wo" and q != CARRIED:
                    pe.wait_ge(y_ready, STREAMS + q + 1)
                elif step == "tr":
                    stage = "ln_out" if kind == "front" else "rms_hat"
                    pe.wait_ge(done[stage], plan.count[stage, key])
                elif step in ("proj", "proj_v", "proj_tok", "fc0", "fc1"):
                    b, u = plan.use["tr", key]
                    pe.wait_ge(front_read[b], u)
                elif step == "tr_qk":
                    pe.wait_ge(done["rope_add"], plan.count["rope_add", key])
                elif step == "pj":
                    pe.wait_ge(done["square1"], plan.count["square1", key])
                if use > 1:
                    pe.wait_ge(front_read[bank], use - 1)
                layer = 0 if kind == "front" else 1
                if step in ("perm", "tr", "wo", "pj", "proj_tok"):
                    for t in range(TILES):
                        cols = slice(t * P, (t + 1) * P)
                        if step == "perm":
                            mm = pe.transpose(dst[:, cols], y_t[q][:, cols], const("perm"))
                        elif step == "tr":
                            mm = pe.transpose(dst[:, cols], x_hat[q][:, t, :], ident)
                        elif step == "wo":
                            mm = pe.matmul(dst[:, cols], y_t[q][:, cols], wo_t[:], start=(t == 0), stop=True, skip_group_check=True)
                        elif step == "proj_tok":
                            pe.matmul(dst[:, cols], x_t[q][:, cols], wqk_t[:, 0:P], start=(t == 0), stop=True, skip_group_check=True)
                            mm = pe.matmul(dst[:, SEQ + t * 32:SEQ + (t + 1) * 32], x_t[q][:, cols], wqk_t[:, P:], start=False, stop=True, skip_group_check=True)
                        else:
                            for h in range(4):
                                mm = pe.matmul(dst[:, cols], hid_t[:, h, cols], w_pj[:, h, :], start=(t == 0 and h == 0), stop=(h == 3), skip_group_check=True)
                elif step == "proj":
                    pe.matmul(dst[:, 0:SEQ], wk_t[:], x_t[q][:], start=True, stop=True, skip_group_check=True)
                    mm = pe.matmul(dst[:, SEQ:], wq_t[:], x_t[q][:], start=False, stop=True, skip_group_check=True)
                elif step == "tr_qk":
                    for t in range(2 * TILES):
                        mm = pe.transpose(dst[:, t * P:(t + 1) * P], rot[:, t * P:(t + 1) * P], ident)
                elif step == "proj_v":
                    for s in range(STRIPS):
                        for j in range(QUADS):
                            mm = pe.matmul(dst[32 * j:32 * j + 32, s * 32:s * 32 + 32], x_t[q][:, STRIP * s:STRIP * s + STRIP],
                                           wv_t[layer][:, 32 * j:32 * j + 32], start=True, stop=True, skip_group_check=True)
                else:
                    for i in range(2):
                        h = 2 * int(step[-1]) + i
                        mm = pe.matmul(dst[:, i * SEQ:(i + 1) * SEQ], w_fc[:, h * P:(h + 1) * P], x_t[q][:], start=(i == 0), stop=True, skip_group_check=True)
                mm.then_inc(front_full[bank], 1)

            for tick in range(plan.ticks):
                for i, core, u in plan.maxima_at(tick):
                    if u < NS:
                        scores(i, core, u)
                for _, core, u, pr in plan.products_at(tick):
                    if u is not None:
                        scores_t(core, u)
                    if pr is not None:
                        product(core, pr)
                for i, _, u in plan.maxima_at(tick):
                    if u == NS + 1:
                        pe.wait_ge(m_ready, i + 1)
                        use = i * S_USES + NS
                        pe.wait_ge(s_read, use - S_RING + 1)
                        pe.transpose(score[0:64, use % S_RING, 0:64].bitcast(BF16), mx_parts[:].rearrange("p t n -> p (t n)"), ident_b[:]).then_inc(s_done, 1)
                for step, key in plan.at(tick, "pe"):
                    if key[0] == "fold":
                        tensor_fold(pe, step)
                    else:
                        step_of(step, key)

        def clear_turn():
            with nc.Block() as block:
                @block.sync
                def _(sp):
                    for s in turn_sems[0::5]:
                        sp.sem_clear(s)

                @block.gpsimd
                def _(pool):
                    for s in turn_sems[1::5]:
                        pool.sem_clear(s)

                @block.scalar
                def _(act):
                    for s in turn_sems[2::5]:
                        act.sem_clear(s)

                @block.vector
                def _(dve):
                    for s in turn_sems[3::5]:
                        dve.sem_clear(s)

                @block.tensor
                def _(pe):
                    for s in turn_sems[4::5]:
                        pe.sem_clear(s)

        x_flat = io["x"].rearrange("b n e -> (b n) e")
        o_flat = out.rearrange("b n e -> (b n) e")

        def rows_at(ap, at):
            return ap[bass.ds(at, SEQ)].rearrange("(t p) e -> p t e", p=P)

        with nc.Block() as block:
            @block.sync
            def _(sp):
                sync_setup(sp)
                sync_program(sp, PROLOGUE, None, None)
                sp.wait_ge(neg_in, 16 * 2 * STREAMS)

            @block.gpsimd
            def _(pool):
                pool_setup(pool)
                pool_program(pool, PROLOGUE)

            @block.scalar
            def _(act):
                scalar_setup(act)
                scalar_program(act, PROLOGUE)

            @block.vector
            def _(dve):
                vector_setup(dve)
                vector_program(dve, PROLOGUE)

            @block.tensor
            def _(pe):
                tensor_setup(pe)
                tensor_program(pe, PROLOGUE)
        clear_turn()

        with nc.Fori(0, TURNS) as turn:
            here = turn * (STREAMS * SEQ)
            after = (turn * (STREAMS * SEQ) + STREAMS * SEQ) % (BATCH * SEQ)
            x_rows = [rows_at(x_flat, after + q * SEQ) for q in range(STREAMS)]
            before = (turn * (STREAMS * SEQ) + (BATCH - STREAMS) * SEQ) % (BATCH * SEQ)
            o_rows = [rows_at(o_flat, (before if q == CARRIED else here) + q * SEQ) for q in range(STREAMS)]
            with nc.Block() as block:
                @block.sync
                def _(sp):
                    sync_program(sp, LOOP, x_rows, o_rows)

                @block.gpsimd
                def _(pool):
                    pool_program(pool, LOOP)

                @block.scalar
                def _(act):
                    scalar_program(act, LOOP)

                @block.vector
                def _(dve):
                    vector_program(dve, LOOP)

                @block.tensor
                def _(pe):
                    tensor_program(pe, LOOP)
            clear_turn()

        with nc.Block() as block:
            @block.sync
            def _(sp):
                sync_program(sp, EPILOGUE, None, [rows_at(o_flat, (BATCH - STREAMS + q) * SEQ) for q in range(STREAMS)])

            @block.gpsimd
            def _(pool):
                pool_program(pool, EPILOGUE)

            @block.scalar
            def _(act):
                scalar_program(act, EPILOGUE)

            @block.vector
            def _(dve):
                vector_program(dve, EPILOGUE)

            @block.tensor
            def _(pe):
                tensor_program(pe, EPILOGUE)


_INS = {"x": "L0_attn_x", "gamma": "L0_attn_gamma", "beta": "L0_attn_beta", "w_qkv": "L0_attn_w_qkv",
        "wq": "L0_ffn_wq", "wk": "L0_ffn_wk", "wv": "L0_ffn_wv", "wo": "L0_ffn_wo",
        "q_gain": "L0_ffn_q_gain", "k_gain": "L0_ffn_k_gain",
        "fc_s1": "L0_ffn_fc_s1", "fc_s2": "L0_ffn_fc_s2", "fc_mix": "L0_ffn_fc_mix", "fc_logits": "L0_ffn_fc_logits",
        "pj_s1": "L0_ffn_pj_s1", "pj_s2": "L0_ffn_pj_s2", "pj_mix": "L0_ffn_pj_mix", "pj_logits": "L0_ffn_pj_logits"}


def _constants():
    import numpy as np

    c = np.zeros((P, CONST_COLS), np.float32)

    def part(name):
        return c[:, CONSTS[name][0]:CONSTS[name][1]]

    rows = np.arange(P)
    part("ident")[:] = np.eye(P, dtype=np.float32)
    g, j, d = rows // 32, rows % 32 // D, rows % D
    part("perm")[rows, 32 * j + D * g + d] = 1.0
    col = np.arange(STRIP)
    part("mask_s")[:] = np.where(col[None, :] > (rows % STRIP)[:, None], -3e38, 0.0)
    part("mask_st")[:] = np.where((rows % STRIP)[:, None] > col[None, :], -3e38, 0.0)
    part("quad")[:] = (rows // D % QUADS)[:, None] == np.arange(QUADS)[None, :]
    part("ones_bd")[:] = (rows // STRIP)[:, None] == (col // D)[None, :]
    part("negsel")[ROWS:MROWS] = -((rows // STRIP)[None, :] == np.arange(QUADS)[:, None]).astype(np.float32)
    t = np.arange(SEQ, dtype=np.float32)
    inv = (1.0 / np.float32(10000.0) ** (np.arange(0, D, 2, dtype=np.float32) / np.float32(D))).astype(np.float32)
    place = np.arange(TILES)[None, :] * P + rows[:, None]
    angle = np.outer(t, inv).astype(np.float32)[place]
    part("cos")[:] = np.concatenate([np.cos(angle), np.cos(angle)], -1).reshape(P, TILES * D)
    part("sin")[:] = np.concatenate([np.sin(angle), -np.sin(angle)], -1).reshape(P, TILES * D)
    part("ones")[:] = 1.0
    return c


def kernel(**inputs):
    import numpy as _np
    import concourse.bacc as _bacc
    from concourse import mybir as _mybir
    from concourse.bass_utils import run_bass_kernel_spmd as _run

    nc = _bacc.Bacc("TRN2", target_bir_lowering=False, num_devices=1)
    arrays, io = {}, {}
    for name, given in _INS.items():
        a = _np.ascontiguousarray(inputs[given])
        arrays[f"in_{name}"] = a
        io[name] = nc.dram_tensor(f"in_{name}", a.shape, _mybir.dt.from_np(a.dtype), kind="ExternalInput").ap()
    arrays["in_consts"] = _constants()
    io["consts"] = nc.dram_tensor("in_consts", (P, CONST_COLS), _mybir.dt.float32, kind="ExternalInput").ap()
    out = nc.dram_tensor("out_x", (BATCH, SEQ, E), _mybir.dt.float32, kind="ExternalOutput").ap()
    build(nc, io, out)
    r = _run(nc, [arrays], core_ids=[0])
    return r.results[0]["out_x"]
```
